# Optimizing a Trainium2 kernel written in Bass

```python
import numpy as np
import jax
import jax.numpy as jnp

def _softmax(x, axis=-1):
    return jax.nn.softmax(x, axis=axis)

def _gelu(x):
    return jax.nn.gelu(x, approximate=True)

def _silu(x):
    return jax.nn.silu(x)

def _sigmoid(x):
    return jax.nn.sigmoid(x)

def _layernorm(x, axis=-1, eps=1e-05):
    m = jnp.mean(x, axis=axis, keepdims=True)
    v = jnp.var(x, axis=axis, keepdims=True)
    return (x - m) / jnp.sqrt(v + eps)

def _scatter_add(tgt, idx, src, axis=0):
    return tgt.at[idx].add(src)

def _segment_sum(src, seg, n):
    return jax.ops.segment_sum(src, seg, n)
kernel_name = 'mk_lm_tower_d1_tok_ids1024_r4_3b4d46'

def setup_inputs(seed: int=0):
    np.random.seed(seed)
    _w = jnp.asarray

    def _rec_inputs():
        import jax
        import jax.numpy as jnp
        _rk = jax.random.key(seed)
        x = jax.random.randint(jax.random.fold_in(_rk, 1), (16, 256), 0, 31983, jnp.int32)
        return x
    x = _rec_inputs()

    def _L0_tok_setup():
        import jax, jax.numpy as jnp
        import numpy as np
        LN_EPS = 1e-05

        def _layernorm(x, gamma, beta):
            mu = jnp.mean(x, axis=-1, keepdims=True)
            var = jnp.mean((x - mu) ** 2, axis=-1, keepdims=True)
            return (x - mu) / jnp.sqrt(var + LN_EPS) * gamma + beta
        key = jax.random.key(seed)
        ks = jax.random.split(key, 12)
        B, S, D, V, H = (2, 512, 256, 8000, 16)
        d_ff = 4 * D
        inp = {}
        inp['V'] = jax.random.randint(ks[0], (B, S), 0, V, dtype=jnp.int64)
        inp['num_heads'] = H
        sc = 0.02
        inp['emb'] = jax.random.normal(ks[1], (V, D), dtype=jnp.float32) * sc
        inp['w_o'] = jax.random.normal(ks[2], (D, D), dtype=jnp.float32) * sc
        inp['w1'] = jax.random.normal(ks[3], (D, d_ff), dtype=jnp.float32) * sc
        inp['b1'] = jnp.zeros((d_ff,), dtype=jnp.float32)
        inp['w2'] = jax.random.normal(ks[4], (d_ff, D), dtype=jnp.float32) * sc
        inp['b2'] = jnp.zeros((D,), dtype=jnp.float32)
        inp['gamma1'] = jnp.ones((D,), dtype=jnp.float32)
        inp['beta1'] = jnp.zeros((D,), dtype=jnp.float32)
        inp['gamma2'] = jnp.ones((D,), dtype=jnp.float32)
        inp['beta2'] = jnp.zeros((D,), dtype=jnp.float32)
        return inp
    _L0_tok_all = _L0_tok_setup()
    _L0_tok_in = {k: v for k, v in _L0_tok_all.items() if k in ('emb', 'w_o', 'w1', 'b1', 'w2', 'b2', 'gamma1', 'beta1', 'gamma2', 'beta2')}
    del _L0_tok_all

    def _L0_attn_setup():
        import jax, jax.numpy as jnp
        import numpy as np
        B, S, D, H = (4, 512, 256, 16)
        DH = D // H
        key = jax.random.key(seed)
        ks = jax.random.split(key, 9)
        sc = 0.02
        return {'x': jax.random.normal(ks[0], (B, S, D), jnp.float32), 'WQ': jax.random.normal(ks[1], (D, D), jnp.float32) * sc, 'bQ': jax.random.normal(ks[2], (D,), jnp.float32) * sc, 'WK': jax.random.normal(ks[3], (D, D), jnp.float32) * sc, 'bK': jax.random.normal(ks[4], (D,), jnp.float32) * sc, 'WV': jax.random.normal(ks[5], (D, D), jnp.float32) * sc, 'bV': jax.random.normal(ks[6], (D,), jnp.float32) * sc, 'WO': jax.random.normal(ks[7], (DH, D), jnp.float32) * sc, 'bO': jax.random.normal(ks[8], (D,), jnp.float32) * sc}
    _L0_attn_all = _L0_attn_setup()
    _L0_attn_in = {k: v for k, v in _L0_attn_all.items() if k in ('WQ', 'bQ', 'WK', 'bK', 'WV', 'bV', 'WO', 'bO')}
    del _L0_attn_all

    def _L0_ffn_setup():
        import jax, jax.numpy as jnp
        import numpy as np

        def _moe_forward(x, Wg, W1, b1, W2, b2):
            B, S, H = x.shape
            E = Wg.shape[1]
            tokens = x.reshape(-1, H)
            T = tokens.shape[0]
            C = -(-T // E)
            logits = tokens @ Wg
            gates = jax.nn.softmax(logits, axis=-1)
            idx = jnp.argmax(gates, axis=1)
            mask1 = jax.nn.one_hot(idx, E, dtype=gates.dtype)
            locations1 = jnp.cumsum(mask1, axis=0) - 1.0
            mask1 = mask1 * (locations1 < C).astype(gates.dtype)
            loc_s = jnp.sum(locations1 * mask1, axis=1).astype(jnp.int32)
            gates1 = jnp.sum(gates * mask1, axis=1)
            loc_oh = jax.nn.one_hot(loc_s, C, dtype=gates.dtype)
            dispatch = mask1[:, :, None] * loc_oh[:, None, :]
            combine = gates1[:, None, None] * dispatch
            expert_in = jnp.einsum('tec,th->ech', dispatch, tokens)
            hidden = jax.nn.relu(jnp.einsum('ech,ehf->ecf', expert_in, W1) + b1[:, None, :])
            expert_out = jnp.einsum('ecf,efh->ech', hidden, W2) + b2[:, None, :]
            out = jnp.einsum('tec,ech->th', combine, expert_out)
            return out.reshape(B, S, H)
        key = jax.random.key(seed)
        ks = jax.random.split(key, 6)
        B, S, H, F, E = (4, 512, 256, 1024, 8)
        x = jax.random.normal(ks[0], (B, S, H), dtype=jnp.float32)
        Wg = jax.random.normal(ks[1], (H, E), dtype=jnp.float32) * (1.0 / np.sqrt(H))
        W1 = jax.random.normal(ks[2], (E, H, F), dtype=jnp.float32) * (1.0 / np.sqrt(H))
        b1 = jnp.zeros((E, F), dtype=jnp.float32)
        W2 = jax.random.normal(ks[3], (E, F, H), dtype=jnp.float32) * (1.0 / np.sqrt(F))
        b2 = jnp.zeros((E, H), dtype=jnp.float32)
        return {'x': x, 'Wg': Wg, 'W1': W1, 'b1': b1, 'W2': W2, 'b2': b2}
    _L0_ffn_all = _L0_ffn_setup()
    _L0_ffn_in = {k: v for k, v in _L0_ffn_all.items() if k in ('Wg', 'W1', 'b1', 'W2', 'b2')}
    del _L0_ffn_all
    return {'x': x, 'L0_tok_emb': _L0_tok_in['emb'], 'L0_tok_w_o': _L0_tok_in['w_o'], 'L0_tok_w1': _L0_tok_in['w1'], 'L0_tok_b1': _L0_tok_in['b1'], 'L0_tok_w2': _L0_tok_in['w2'], 'L0_tok_b2': _L0_tok_in['b2'], 'L0_tok_gamma1': _L0_tok_in['gamma1'], 'L0_tok_beta1': _L0_tok_in['beta1'], 'L0_tok_gamma2': _L0_tok_in['gamma2'], 'L0_tok_beta2': _L0_tok_in['beta2'], 'L0_attn_WQ': _L0_attn_in['WQ'], 'L0_attn_bQ': _L0_attn_in['bQ'], 'L0_attn_WK': _L0_attn_in['WK'], 'L0_attn_bK': _L0_attn_in['bK'], 'L0_attn_WV': _L0_attn_in['WV'], 'L0_attn_bV': _L0_attn_in['bV'], 'L0_attn_WO': _L0_attn_in['WO'], 'L0_attn_bO': _L0_attn_in['bO'], 'L0_ffn_Wg': _L0_ffn_in['Wg'], 'L0_ffn_W1': _L0_ffn_in['W1'], 'L0_ffn_b1': _L0_ffn_in['b1'], 'L0_ffn_W2': _L0_ffn_in['W2'], 'L0_ffn_b2': _L0_ffn_in['b2']}

def reference(x, L0_tok_emb, L0_tok_w_o, L0_tok_w1, L0_tok_b1, L0_tok_w2, L0_tok_b2, L0_tok_gamma1, L0_tok_beta1, L0_tok_gamma2, L0_tok_beta2, L0_attn_WQ, L0_attn_bQ, L0_attn_WK, L0_attn_bK, L0_attn_WV, L0_attn_bV, L0_attn_WO, L0_attn_bO, L0_ffn_Wg, L0_ffn_W1, L0_ffn_b1, L0_ffn_W2, L0_ffn_b2):
    import jax
    import jax.numpy as jnp

    def _L0_tok_ref(V, num_heads, emb, w_o, w1, b1, w2, b2, gamma1, beta1, gamma2, beta2):
        import jax, jax.numpy as jnp
        import numpy as np
        LN_EPS = 1e-05

        def _layernorm(x, gamma, beta):
            mu = jnp.mean(x, axis=-1, keepdims=True)
            var = jnp.mean((x - mu) ** 2, axis=-1, keepdims=True)
            return (x - mu) / jnp.sqrt(var + LN_EPS) * gamma + beta
        x = emb[V]
        B, S, D = x.shape
        hd = D // num_heads
        qh = x.reshape(B, S, num_heads, hd)
        scores = jnp.einsum('bqhd,bkhd->bhqk', qh, qh) / jnp.sqrt(jnp.float32(hd))
        attn = jax.nn.softmax(scores, axis=-1)
        ctx = jnp.einsum('bhqk,bkhd->bqhd', attn, qh).reshape(B, S, D)
        attn_out = ctx @ w_o
        x1 = _layernorm(x + attn_out, gamma1, beta1)
        ff = jax.nn.relu(x1 @ w1 + b1) @ w2 + b2
        return _layernorm(x1 + ff, gamma2, beta2)

    def _L0_attn_ref(x, WQ, bQ, WK, bK, WV, bV, WO, bO):
        import jax, jax.numpy as jnp
        import numpy as np
        B, S, D, H = (4, 512, 256, 16)
        DH = D // H
        b, s, d = x.shape
        h, dh = (H, DH)
        Q = (x @ WQ + bQ).reshape(b, s, h, dh).transpose(0, 2, 1, 3)
        K = (x @ WK + bK).reshape(b, s, h, dh).transpose(0, 2, 1, 3)
        V = (x @ WV + bV).reshape(b, s, h, dh).transpose(0, 2, 1, 3)
        scale = jnp.sqrt(jnp.float32(dh))
        scores = jnp.einsum('bhqd,bhkd->bhqk', Q, K) / scale
        causal = jnp.tril(jnp.ones((s, s), dtype=bool))
        scores = jnp.where(causal, scores, jnp.float32(-100000.0))
        A = jax.nn.softmax(scores, axis=-1)
        Z = jnp.einsum('bhqk,bhkd->bhqd', A, V)
        out = jnp.einsum('bhsd,de->bse', Z, WO) + jnp.float32(h) * bO
        return out

    def _L0_ffn_ref(x, Wg, W1, b1, W2, b2):
        import jax, jax.numpy as jnp
        import numpy as np

        def _moe_forward(x, Wg, W1, b1, W2, b2):
            B, S, H = x.shape
            E = Wg.shape[1]
            tokens = x.reshape(-1, H)
            T = tokens.shape[0]
            C = -(-T // E)
            logits = tokens @ Wg
            gates = jax.nn.softmax(logits, axis=-1)
            idx = jnp.argmax(gates, axis=1)
            mask1 = jax.nn.one_hot(idx, E, dtype=gates.dtype)
            locations1 = jnp.cumsum(mask1, axis=0) - 1.0
            mask1 = mask1 * (locations1 < C).astype(gates.dtype)
            loc_s = jnp.sum(locations1 * mask1, axis=1).astype(jnp.int32)
            gates1 = jnp.sum(gates * mask1, axis=1)
            loc_oh = jax.nn.one_hot(loc_s, C, dtype=gates.dtype)
            dispatch = mask1[:, :, None] * loc_oh[:, None, :]
            combine = gates1[:, None, None] * dispatch
            expert_in = jnp.einsum('tec,th->ech', dispatch, tokens)
            hidden = jax.nn.relu(jnp.einsum('ech,ehf->ecf', expert_in, W1) + b1[:, None, :])
            expert_out = jnp.einsum('ecf,efh->ech', hidden, W2) + b2[:, None, :]
            out = jnp.einsum('tec,ech->th', combine, expert_out)
            return out.reshape(B, S, H)
        return _moe_forward(x, Wg, W1, b1, W2, b2)
    h = _L0_tok_ref(x, 16, L0_tok_emb, L0_tok_w_o, L0_tok_w1, L0_tok_b1, L0_tok_w2, L0_tok_b2, L0_tok_gamma1, L0_tok_beta1, L0_tok_gamma2, L0_tok_beta2)
    h = h + _L0_attn_ref(_layernorm(h, axis=-1), L0_attn_WQ, L0_attn_bQ, L0_attn_WK, L0_attn_bK, L0_attn_WV, L0_attn_bV, L0_attn_WO, L0_attn_bO)
    h = h + _L0_ffn_ref(_layernorm(h, axis=-1), L0_ffn_Wg, L0_ffn_W1, L0_ffn_b1, L0_ffn_W2, L0_ffn_b2)
    return h

_drawn_inputs = setup_inputs


def setup_inputs(seed=0):
    import zlib

    import numpy as np

    out = dict(_drawn_inputs(seed))
    spreads = {'L0_tok_b1': (0.0, 0.1),
     'L0_tok_b2': (0.0, 0.1),
     'L0_tok_gamma1': (1.0, 0.2),
     'L0_tok_beta1': (0.0, 0.1),
     'L0_tok_gamma2': (1.0, 0.2),
     'L0_tok_beta2': (0.0, 0.1),
     'L0_ffn_b1': (0.0, 0.45),
     'L0_ffn_b2': (0.0, 0.337)}
    factors = {'L0_attn_WQ': 8.0,
     'L0_attn_bQ': 37.32,
     'L0_attn_WK': 8.0,
     'L0_attn_bK': 64.0,
     'L0_attn_bV': 5.356}
    for name, (base, spread) in spreads.items():
        noise = np.random.default_rng([zlib.crc32(name.encode()), seed]).standard_normal(out[name].shape)
        drawn = base * np.exp(spread * noise) if base else spread * noise
        out[name] = jnp.asarray(drawn.astype(out[name].dtype))
    for name, factor in factors.items():
        out[name] = (out[name] * factor).astype(out[name].dtype)
    return out
```

```python
from contextlib import ExitStack

import concourse.bass as bass
from concourse import mybir

P = 128
ALU = mybir.AluOpType
ACT = mybir.ActivationFunctionType
F32 = mybir.dt.float32
F32R = mybir.dt.float32r
BF16 = mybir.dt.bfloat16
I32 = mybir.dt.int32
AX_X = mybir.AxisListType.X

EPS = 1e-5
MASKED = -400000.0
HEADS = 16
ROW_EXTRA = 4
DMA = 16
NEWTON = 3
VECTOR_LINKS = 80
POOL_LINKS = 4


def lm_tower_kernel(nc, x, emb, w_o, w1, b1, w2, b2, gamma1, beta1, gamma2, beta2,
                    WQ, bQ, WK, bK, WV, bV, WO, bO, Wg, mW1, mb1, mW2, mb2, out):
    B, S = x.shape
    V, D = emb.shape
    F = w1.shape[1]
    E, _, MF = mW1.shape
    H = HEADS
    HD = D // H
    T = S // P
    C2 = D // P
    NF = F // P
    N = B * S
    CAP = -(-N // E)
    CT = CAP // P
    G = H // 4
    ROW = D + ROW_EXTRA
    NT = N // P
    assert (T, C2, NF, HD, CT, G) == (2, 2, 8, 16, 4, 4) and MF == F
    NOWHERE = 1 << 20
    SCALE = float(HD) ** -0.5

    slots_dram = nc.dram_tensor("expert_slots", [E * CAP, ROW], F32).ap()

    with ExitStack() as ctx:
        def sb(name, shape, dt=F32):
            return ctx.enter_context(nc.sbuf_tensor(name, shape, dt))

        def sem(name):
            return ctx.enter_context(nc.semaphore(name))

        def psum(name, shape):
            return ctx.enter_context(nc.psum_tensor(name, shape, F32))

        wide = psum("wide", [P, 4, 512])
        bank = [psum("bank0", [P, 512])[:], psum("bank1", [P, 512])[:], *(wide[:, k, :] for k in range(4)),
                psum("bank6", [P, 512])[:], psum("bank7", [P, 512])[:]]

        ident = sb("ident", [P, P])
        identb = sb("identb", [P, P], BF16)
        maskq = sb("maskq", [P, P], BF16)
        maskk = sb("maskk", [P, P], BF16)
        before = sb("before", [P, P], BF16)
        onesb = sb("onesb", [P, P], BF16)
        zerob = sb("zerob", [P, P], BF16)
        sel16 = sb("sel16", [P, 4])
        mask16 = sb("mask16", [P, 1])
        w_o_sb = sb("w_o_sb", [P, C2, D])
        w1_sb = sb("w1_sb", [P, C2, F])
        w2_sb = sb("w2_sb", [P, NF, D])
        wv_sb = sb("wv_sb", [P, C2, D])
        wstage = sb("wstage", [P, 2, C2, D])
        wqk = sb("wqk", [P, 2, C2, H, 32])
        wg_sb = sb("wg_sb", [P, C2, E])
        wo_sb = sb("wo_sb", [HD, D])
        b1_sb = sb("b1_sb", [P, NF])
        bqk = sb("bqk", [P, 2, G])
        g1c = sb("g1c", [P, C2])
        be1c = sb("be1c", [P, C2])
        rows = sb("rows", [P, 7, D])
        be1b2 = sb("be1b2", [P, D])
        bo16 = sb("bo16", [P, D])
        ids_i = sb("ids_i", [NT, P], I32)
        ids_f = sb("ids_f", [NT, P])
        ids_n = sb("ids_n", [NT, P])
        idx_all = sb("idx_all", [P, NT + T], I32)
        ebase = sb("ebase", [P, T, E])
        rev = sb("rev", [P, T, E])
        empty = sb("empty", [P, ROW])

        gidx = sb("gidx", [P, T], I32)
        xg = sb("xg", [P, T, D])
        xpad = sb("xpad", [P, T, H, 32])
        vpad = sb("vpad", [P, T, H, 32])
        negmax = sb("negmax", [P, T, H, 32])
        KT = {s: sb(f"KT_{s}", [P, G, S]) for s in ("tok", "att")}
        KH = {s: sb(f"KH_{s}", [P, G, S], F32R) for s in ("tok", "att")}
        Q0 = sb("Q0", [P, G, S])
        QH = sb("QH", [P, G, S], F32R)
        QT = sb("QT", [P, G, S])
        rowmax = sb("rowmax", [P, T, H])
        blockmax = sb("blockmax", [P, 3, H])
        prob = sb("prob", [P, 2, 4, 512])
        CU = sb("CU", [P, G, S])
        recip = sb("recip", [P, T, H])
        ctxn = sb("ctxn", [P, T, H, HD])
        featT = sb("featT", [P, C2, S])
        hid = sb("hid", [P, NF, CAP])
        resid = sb("resid", [P, T, D])
        normed = sb("normed", [P, T, D])
        scaled = sb("scaled", [P, T, D])
        x1b = sb("x1b", [P, T, D])
        h1 = sb("h1", [P, T, D])
        h1b = sb("h1b", [P, T, D])
        stats = sb("stats", [P, T, 6])
        mv = sb("mv", [P, T, 2])
        rstd = sb("rstd", [P, T])
        var = sb("var", [P, T])
        halved = sb("halved", [P, T], I32)
        corr = sb("corr", [P, T])
        zsum = sb("zsum", [P, T, HD])
        zT = sb("zT", [HD, S])
        h2row = sb("h2row", [P, T, ROW])
        tokid = sb("tokid", [P, T], I32)
        lg = sb("lg", [P, T, E])
        lmax = sb("lmax", [P, T])
        lsh = sb("lsh", [P, T, E])
        lexp = sb("lexp", [P, T, E])
        lsum = sb("lsum", [P, T])
        eq = sb("eq", [P, T, E])
        eqr = sb("eqr", [P, T, E])
        first = sb("first", [P, T])
        onehot = sb("onehot", [P, T, E])
        onehotb = sb("onehotb", [P, T, E], BF16)
        posr = sb("posr", [P, T, E])
        sel = sb("sel", [P, T, E])
        locf = sb("locf", [P, T])
        slotf = sb("slotf", [P, T])
        over = sb("over", [P, T])
        sloti = sb("sloti", [P, T], I32)
        counts = sb("counts", [P, E])
        xe = sb("xe", [P, 2, CT, ROW])
        xen = CU[:]
        xeT = sb("xeT", [P, C2, CAP])
        mw1 = sb("mw1", [P, 2, C2, MF])
        mw2 = sb("mw2", [P, 2, NF, D])
        mb1_sb = sb("mb1_sb", [P, 2, NF])
        mb2_sb = sb("mb2_sb", [P, 2, D])
        yb = sb("yb", [P, 2, D])
        yo = prob[:, :, :, 0:D]

        loaded = sem("loaded")
        ids_loaded = sem("ids_loaded")
        pool_const = sem("pool_const")
        vec_const = sem("vec_const")
        ids_cleaned = sem("ids_cleaned")
        ids_turned = sem("ids_turned")
        ids_ready = sem("ids_ready")
        gathered = sem("gathered")
        x_padded = sem("x_padded")
        x_turned = sem("x_turned")
        vector_step = sem("vector_step")
        pool_step = sem("pool_step")
        core = {}
        for s in ("tok", "att"):
            core[s] = {k: sem(f"{s}_{k}") for k in (
                "keysT", "keys_rounded", "scores", "maxed", "neg_ready", "neg_turned", "queries",
                "scoresT", "probs", "ctx_done", "ctx_copied", "ctx_turned", "ctx_normed")}
        q_ready = sem("q_ready")
        q_rounded = sem("q_rounded")
        ctxn_turned = sem("ctxn_turned")
        ctxnT_ready = sem("ctxnT_ready")
        attn_out = sem("attn_out")
        x1_normed = sem("x1_normed")
        x1_turned = sem("x1_turned")
        x1T_ready = sem("x1T_ready")
        x1b_ready = sem("x1b_ready")
        up_done = sem("up_done")
        relu_act = sem("relu_act")
        relu_dve = sem("relu_dve")
        down_done = sem("down_done")
        y_normed = sem("y_normed")
        h1_ready = sem("h1_ready")
        h1_normed = sem("h1_normed")
        h1_turned = sem("h1_turned")
        h1T_ready = sem("h1T_ready")
        h1b_ready = sem("h1b_ready")
        k_proj = sem("k_proj")
        q_proj = sem("q_proj")
        v_proj = sem("v_proj")
        v_ready = sem("v_ready")
        z_ready = sem("z_ready")
        z_turned = sem("z_turned")
        zT_ready = sem("zT_ready")
        z_out = sem("z_out")
        h2_ready = sem("h2_ready")
        h2_normed = sem("h2_normed")
        h2_turned = sem("h2_turned")
        h2T_ready = sem("h2T_ready")
        logits = sem("logits")
        shifted = sem("shifted")
        exped = sem("exped")
        onehot_ready = sem("onehot_ready")
        ranked = sem("ranked")
        slot_ready = sem("slot_ready")
        tokid_ready = sem("tokid_ready")
        out_stored = sem("out_stored")
        scattered = sem("scattered")
        e_loaded = [sem("e_loaded0"), sem("e_loaded1")]
        e_normed = sem("e_normed")
        e_turned = sem("e_turned")
        eT_ready = sem("eT_ready")
        e_up = sem("e_up")
        e_relu = sem("e_relu")
        e_down = sem("e_down")
        e_biased = sem("e_biased")
        e_out = sem("e_out")
        e_scattered = [sem("e_scattered0"), sem("e_scattered1")]

        PRODUCTS = {"tok": [(t, t * S, S) for t in range(T)], "att": [(t, t * P, (t + 1) * P) for t in range(T)]}

        tok_rows = out.rearrange("b (t p) d -> b p t d", p=P)
        flat_out = out.rearrange("b s d -> (b s) d")

        passed = sem("passed")

        def wait_apart(eng, semaphore, value):
            eng.wait_ge(semaphore, value)
            eng.sem_inc(passed, 1)

        block = ctx.enter_context(nc.Block())

        N_LOADS = 28
        UP = (2, 3, 5, 7)
        QB = (5, 7)

        @block.sync
        def _(sp):
            sp.dma_start(ids_i[:], x.rearrange("b (t p) -> (b t) p", p=P)).then_inc(ids_loaded, DMA)

            def load(dst, src):
                sp.dma_start(dst, src).then_inc(loaded, DMA)

            for c in range(C2):
                load(wstage[:, 0, c, :], WQ[c * P:(c + 1) * P, :])
                load(wstage[:, 1, c, :], WK[c * P:(c + 1) * P, :])
            with nc.allow_non_contiguous_dma(reason="a few bias columns"):
                load(b1_sb[:], b1.rearrange("(f p) -> p f", p=P))
                load(g1c[:], gamma1.rearrange("(c p) -> p c", p=P))
                load(be1c[:], beta1.rearrange("(c p) -> p c", p=P))
            for k, r in enumerate((gamma1, beta1, b2, gamma2, beta2, bV, bO)):
                load(rows[:, k, :], r.rearrange("(a d) -> a d", a=1).to_broadcast([P, D]))
            load(w_o_sb[:], w_o.rearrange("(c p) n -> p c n", p=P))
            load(w1_sb[:], w1.rearrange("(c p) n -> p c n", p=P))
            load(w2_sb[:], w2.rearrange("(c p) n -> p c n", p=P))
            load(wv_sb[:], WV.rearrange("(c p) n -> p c n", p=P))
            load(wo_sb[:], WO)
            load(wg_sb[:], Wg.rearrange("(c p) n -> p c n", p=P))
            sp.wait_ge(pool_const, 5)
            with nc.allow_non_contiguous_dma(reason="padded biases, once"):
                for r in range(4):
                    for k, bias in enumerate((bQ, bK)):
                        sp.dma_start(bqk[32 * r:32 * r + HD, k, :],
                                     bias.rearrange("(g r d) -> r d g", r=4, d=HD)[r]).then_inc(loaded, DMA)

            sp.sem_inc(out_stored, DMA)
            with sp.Fori(0, B, 1) as i:
                sp.wait_ge(h2_ready, i + 1)
                sp.dma_start(tok_rows[i], h2row[:, :, 0:D]).then_inc(out_stored, DMA)

            def load_expert(e, k):
                w = e_loaded[k]
                sp.dma_start(xe[:, k], slots_dram.rearrange("(e t p) r -> e p t r", t=CT, p=P)[e]).then_inc(w, DMA)
                sp.dma_start(mw1[:, k], mW1.rearrange("e (c p) f -> e p c f", p=P)[e]).then_inc(w, DMA)
                sp.dma_start(mw2[:, k], mW2.rearrange("e (c p) f -> e p c f", p=P)[e]).then_inc(w, DMA)
                with nc.allow_non_contiguous_dma(reason="bias columns"):
                    sp.dma_start(mb1_sb[:, k], mb1.rearrange("e (f p) -> e p f", p=P)[e]).then_inc(w, DMA)
                sp.dma_start(mb2_sb[:, k], mb2.rearrange("e (a d) -> e a d", a=1)[e].to_broadcast([P, D])).then_inc(w, DMA)

            sp.wait_ge(scattered, DMA * T * B + DMA)
            load_expert(0, 0)
            load_expert(1, 1)
            with sp.Fori(0, E // 2 - 1, 1) as j:
                for k in range(2):
                    sp.wait_ge(e_scattered[k], (j + 1) * (CT * DMA))
                    load_expert(2 * j + 2 + k, k)

        @block.gpsimd
        def _(pool):
            pool.memset(bqk[:], 0.0).then_inc(pool_const, 1)
            pool.memset(empty[:], 0.0).then_inc(pool_const, 1)
            pool.memset(wqk[:], 0.0).then_inc(pool_const, 1)
            pool.memset(negmax[:], 0.0).then_inc(pool_const, 1)
            pool.wait_ge(pool_const, 4)
            pool.memset(empty[:].bitcast(I32)[:, D + 1:D + 2], NOWHERE).then_inc(pool_const, 1)
            pool.memset(xpad[:], 0.0).then_inc(pool_const, 1)
            pool.memset(vpad[:], 0.0).then_inc(pool_const, 1)
            pool.memset(ident[:], 0.0).then_inc(pool_const, 1)
            pool.memset(onesb[:], 1.0).then_inc(pool_const, 1)
            pool.memset(zerob[:], 0.0).then_inc(pool_const, 1)
            pool.memset(sel16[:], 0.0).then_inc(pool_const, 1)
            pool.memset(idx_all[:], 0).then_inc(pool_const, 1)
            pool.memset(counts[:], 0.0).then_inc(pool_const, 1)
            pool.wait_ge(pool_const, 13)
            pool.memset(xpad[:, :, :, HD:HD + 1], 1.0).then_inc(pool_const, 1)
            pool.memset(vpad[:, :, :, HD:HD + 1], 1.0).then_inc(pool_const, 1)
            pool.affine_select(out=ident[:], in_=ident[:], compare_op=ALU.not_equal, fill=1.0, base=0,
                               pattern=[[-1, P]], channel_multiplier=1).then_inc(pool_const, 1)
            pool.affine_select(out=maskq[:], in_=zerob[:], compare_op=ALU.is_ge, fill=MASKED, base=0,
                               pattern=[[-1, P]], channel_multiplier=1).then_inc(pool_const, 1)
            pool.affine_select(out=maskk[:], in_=zerob[:], compare_op=ALU.is_ge, fill=MASKED, base=0,
                               pattern=[[1, P]], channel_multiplier=-1).then_inc(pool_const, 1)
            pool.affine_select(out=before[:], in_=onesb[:], compare_op=ALU.is_gt, fill=0.0, base=0,
                               pattern=[[1, P]], channel_multiplier=-1).then_inc(pool_const, 1)
            pool.affine_select(out=sel16[:], in_=sel16[:], compare_op=ALU.not_equal, fill=1.0, base=-HD,
                               pattern=[[-32, 4]], channel_multiplier=1).then_inc(pool_const, 1)
            pool.iota(tokid[:], pattern=[[P, T]], base=-S, channel_multiplier=1).then_inc(pool_const, 1)
            pool.iota(ebase[:], pattern=[[0, T], [CAP, E]], base=0, channel_multiplier=0,
                      allow_small_or_imprecise_dtypes=True).then_inc(pool_const, 1)
            pool.iota(rev[:], pattern=[[0, T], [-1, E]], base=E, channel_multiplier=0,
                      allow_small_or_imprecise_dtypes=True).then_inc(pool_const, 1)
            pool.wait_ge(pool_const, 23)
            pool.tensor_copy(identb[:], ident[:]).then_inc(pool_const, 1)

            def gather(i):
                pool.tensor_copy(gidx[:], idx_all[:, bass.ds(i * T, T)]).then_inc(pool_step, 1)

            def issue_gathers(step):
                wait_apart(pool, pool_step, step)
                for t in range(T):
                    pool.indirect_dma_start(xg[:, t, :], None, emb, bass.IndirectOffsetOnAxis(gidx[:, t:t + 1], 0)
                                            ).then_inc(gathered, DMA)

            pool.wait_ge(ids_ready, 1)
            gather(0)
            issue_gathers(1)
            pool.wait_ge(loaded, N_LOADS * DMA)
            for k in range(2):
                pool.tensor_copy(wqk[:, k, :, :, 0:HD],
                                 wstage[:, k].rearrange("p c (h d) -> p c h d", h=H)).then_inc(pool_const, 1)
            pool.dma_start(slots_dram.rearrange("(p s) r -> p s r", p=P),
                           empty[:].rearrange("p (a r) -> p a r", a=1).to_broadcast([P, E * CAP // P, ROW])
                           ).then_inc(scattered, DMA)
            pool.wait_ge(scattered, DMA)

            with pool.Fori(0, B, 1) as i:
                step = i * POOL_LINKS + 1
                wait_apart(pool, gathered, (i + 1) * (T * DMA))
                wait_apart(pool, x1_normed, i + 1)
                pool.tensor_copy(xpad[:, :, :, 0:HD],
                                 xg[:].rearrange("p t (h d) -> p t h d", h=H)).then_inc(x_padded, 1)
                gather(i + 1)
                wait_apart(pool, x_padded, i + 1)
                issue_gathers(step + 1)
                tok = core["tok"]
                for half in range(2):
                    wait_apart(pool, tok["keysT"], i * 2 + half + 1)
                    pool.tensor_copy(KH["tok"][:, 2 * half:2 * half + 2, :],
                                     KT["tok"][:, 2 * half:2 * half + 2, :]).then_inc(tok["keys_rounded"], 1)
                wait_apart(pool, x1_normed, i + 2)
                for t in range(T):
                    ins = pool.tensor_tensor(scaled[:, t, :], normed[:, t, :], rows[:, 0, :], ALU.mult)
                ins.then_inc(pool_step, 1)
                wait_apart(pool, pool_step, step + 2)
                for t in range(T):
                    ins = pool.tensor_tensor(x1b[:, t, :], scaled[:, t, :], be1b2[:], ALU.add)
                ins.then_inc(x1b_ready, 1)
                wait_apart(pool, y_normed, i + 1)
                wait_apart(pool, x1b_ready, i + 1)
                for t in range(T):
                    ins = pool.tensor_tensor(scaled[:, t, :], normed[:, t, :], rows[:, 3, :], ALU.mult)
                ins.then_inc(pool_step, 1)
                wait_apart(pool, pool_step, step + 3)
                for t in range(T):
                    ins = pool.tensor_tensor(h1[:, t, :], scaled[:, t, :], rows[:, 4, :], ALU.add)
                ins.then_inc(h1_ready, 1)
                wait_apart(pool, h1_ready, i + 1)
                for t in range(T):
                    ins = pool.tensor_tensor(h1b[:, t, :], h1[:, t, :], bo16[:], ALU.add)
                ins.then_inc(h1b_ready, 1)
                att = core["att"]
                for half in range(2):
                    wait_apart(pool, att["keysT"], i * G + 2 * half + 2)
                    pool.tensor_copy(KH["att"][:, 2 * half:2 * half + 2, :],
                                     KT["att"][:, 2 * half:2 * half + 2, :]).then_inc(att["keys_rounded"], 1)
                    wait_apart(pool, q_ready, i * G + 2 * half + 2)
                    pool.tensor_copy(QH[:, 2 * half:2 * half + 2, :],
                                     Q0[:, 2 * half:2 * half + 2, :]).then_inc(q_rounded, 1)
                pool.tensor_scalar(tokid[:], tokid[:], float(S), None, ALU.add).then_inc(pool_step, 1)
                wait_apart(pool, pool_step, step + 4)
                wait_apart(pool, scattered, i * (T * DMA) + DMA)
                pool.tensor_copy(h2row[:, :, D + 1:D + 2].bitcast(I32),
                                 tokid[:].rearrange("p (t a) -> p t a", a=1)).then_inc(tokid_ready, 1)
                wait_apart(pool, slot_ready, i + 1)
                wait_apart(pool, tokid_ready, i + 1)
                for t in range(T):
                    pool.indirect_dma_start(slots_dram, bass.IndirectOffsetOnAxis(sloti[:, t:t + 1], 0),
                                            h2row[:, t, :], None, bounds_check=E * CAP - 1,
                                            oob_is_err=False).then_inc(scattered, DMA)

            pool.wait_ge(out_stored, B * DMA + DMA)
            with pool.Fori(0, E // 2, 1) as j:
                for k in range(2):
                    for t in range(CT):
                        wait_apart(pool, e_out, j * (2 * CT) + k * CT + t + 1)
                        pool.indirect_dma_start(flat_out, bass.IndirectOffsetOnAxis(
                            xe[:, k, t, D + 1:D + 2].bitcast(I32), 0), yo[:, k, t, :], None,
                            bounds_check=N - 1, oob_is_err=False).then_inc(e_scattered[k], DMA)
            pool.wait_ge(gathered, (B + 1) * T * DMA)
            for k in range(2):
                pool.wait_ge(e_scattered[k], E // 2 * CT * DMA)

        @block.scalar
        def _(act):
            def attention(s, i):
                c = core[s]
                for step in range(1, G + 2):
                    g = step - 1
                    if g < G:
                        for p in (2 * g, 2 * g + 1):
                            act.wait_ge(c["scoresT"], i * (2 * G) + p + 1)
                            if g >= 2:
                                act.wait_ge(c["ctx_done"], i * G + g - 1)
                            q = 2 * (p % 2)
                            n = 2 * S if s == "tok" else S + P
                            act.activation(prob[:, g % 2, q:q + 2, 0:n], wide[:, q:q + 2, 0:n], ACT.Exp,
                                           scale=SCALE).then_inc(c["probs"], 1)
                    if step >= 2:
                        g = step - 2
                        act.wait_ge(c["ctx_done"], i * G + g + 1)
                        act.activation(CU[:, g, :], bank[6][:, (g % 2) * S:(g % 2 + 1) * S],
                                       ACT.Copy).then_inc(c["ctx_copied"], 1)

            act.wait_ge(loaded, N_LOADS * DMA)
            act.wait_ge(vec_const, 5)
            with act.Fori(0, B, 1) as i:
                for half in range(2):
                    act.wait_ge(x_turned, i * 2 + half + 1)
                    act.activation(KT["tok"][:, 2 * half:2 * half + 2, :], bank[2 + half].rearrange(
                        "p (g q) -> p g q", g=2), ACT.Copy).then_inc(core["tok"]["keysT"], 1)
                attention("tok", i)
                act.wait_ge(ctxn_turned, i + 1)
                act.activation(featT[:], bank[2].rearrange("p (c q) -> p c q", c=C2), ACT.Copy).then_inc(ctxnT_ready, 1)
                act.wait_ge(x1_turned, i + 1)
                for c in range(C2):
                    ins = act.activation(featT[:, c, :], bank[4][:, c * S:(c + 1) * S], ACT.Identity,
                                         bias=be1c[:, c:c + 1], scale=g1c[:, c:c + 1])
                ins.then_inc(x1T_ready, 1)
                for pair_of in range(0, NF // 2, 2):
                    act.wait_ge(up_done, i * (NF // 2) + pair_of + 1)
                    for f in (2 * pair_of, 2 * pair_of + 1):
                        ins = act.activation(hid[:, f, 0:S], bank[UP[pair_of]][:, (f % 2) * S:(f % 2 + 1) * S],
                                             ACT.Relu, bias=b1_sb[:, f:f + 1])
                    ins.then_inc(relu_act, 1)
                act.wait_ge(h1_turned, i + 1)
                act.activation(featT[:], bank[4].rearrange("p (c q) -> p c q", c=C2), ACT.Copy).then_inc(h1T_ready, 1)
                for g in range(G):
                    if g % 2 == 0:
                        act.wait_ge(k_proj, i * (G // 2) + g // 2 + 1)
                    act.activation(KT["att"][:, g, :], bank[2 + g // 2][:, (g % 2) * S:(g % 2 + 1) * S],
                                   ACT.Identity, bias=bqk[:, 1, g:g + 1]).then_inc(core["att"]["keysT"], 1)
                attention("att", i)
                act.wait_ge(z_turned, i + 1)
                act.activation(zT[:], bank[2][0:HD, 0:S], ACT.Copy).then_inc(zT_ready, 1)
                act.wait_ge(h2_turned, i + 1)
                act.activation(featT[:], bank[4].rearrange("p (c q) -> p c q", c=C2), ACT.Copy).then_inc(h2T_ready, 1)
                act.wait_ge(shifted, i + 1)
                act.activation(lexp[:], lsh[:], ACT.Exp).then_inc(exped, 1)
            with act.Fori(0, E // 2, 1) as j:
                for k in range(2):
                    for f in range(NF):
                        act.wait_ge(e_up, j * (2 * NF) + k * NF + f + 1)
                        act.activation(hid[:, f, :], bank[2 + f % 4], ACT.Relu,
                                       bias=mb1_sb[:, k, f:f + 1]).then_inc(e_relu, 1)

        @block.vector
        def _(dve):
            done = [0]

            def const(ins):
                ins.then_inc(vec_const, 1)
                done[0] += 1
                dve.wait_ge(vec_const, done[0])

            dve.sem_inc(x1_normed, 1)
            dve.sem_inc(e_biased, 1)
            dve.wait_ge(pool_const, 23)
            const(dve.tensor_reduce(mask16[:], sel16[:], AX_X, ALU.add))
            dve.wait_ge(ids_loaded, DMA)
            const(dve.tensor_copy(ids_f[:], ids_i[:]))
            const(dve.tensor_scalar(ids_n[:], ids_f[:], 0.0, float(V), ALU.is_lt, ALU.mult))
            const(dve.tensor_tensor(ids_f[:], ids_f[:], ids_n[:], ALU.add))
            dve.wait_ge(loaded, N_LOADS * DMA)
            const(dve.tensor_scalar(bqk[:, 1, :], bqk[:, 1, :], mask16[:, 0:1], None, ALU.add))
            dve.tensor_scalar(ids_f[:], ids_f[:], float(V - 1), 0.0, ALU.min, ALU.max).then_inc(ids_cleaned, 1)
            dve.tensor_tensor(be1b2[:], rows[:, 1, :], rows[:, 2, :], ALU.add).then_inc(vec_const, 1)
            dve.tensor_scalar(bo16[:], rows[:, 6, :], float(H), None, ALU.mult).then_inc(vec_const, 1)
            dve.wait_ge(ids_turned, 1)
            dve.tensor_copy(idx_all[:, 0:NT], bank[7][:, 0:NT]).then_inc(ids_ready, 1)

            base = [None, 0]

            def link(ins, apart=False):
                base[1] += 1
                ins.then_inc(vector_step, 1)
                if apart:
                    wait_apart(dve, vector_step, base[0] * VECTOR_LINKS + base[1])
                else:
                    dve.wait_ge(vector_step, base[0] * VECTOR_LINKS + base[1])

            def moments(src):
                for t in range(T):
                    ins = dve.bn_stats(stats[:, t, :], src[:, t, 0:D])
                link(ins, apart=True)
                for t in range(T):
                    ins = dve.bn_aggr(mv[:, t, :], stats[:, t, :])
                link(ins)
                link(dve.tensor_scalar(var[:], mv[:, :, 1], EPS, None, ALU.add))
                link(dve.tensor_scalar(halved[:], var[:].bitcast(I32), 1, None, ALU.logical_shift_right))
                link(dve.tensor_scalar(rstd[:].bitcast(I32), halved[:], -1.0, float(0x5F3759DF), ALU.mult, ALU.add))
                for _ in range(NEWTON):
                    link(dve.scalar_tensor_tensor(out=corr[:], in0=rstd[:], scalar=-0.5, in1=rstd[:],
                                                  op0=ALU.mult, op1=ALU.mult))
                    link(dve.tensor_tensor(corr[:], corr[:], var[:], ALU.mult))
                    link(dve.scalar_tensor_tensor(out=rstd[:], in0=corr[:], scalar=1.5, in1=rstd[:],
                                                  op0=ALU.add, op1=ALU.mult))

            def normalise(src):
                moments(src)
                for t in range(T):
                    ins = dve.tensor_scalar(normed[:, t, :], src[:, t, 0:D], mv[:, t, 0:1], rstd[:, t:t + 1],
                                            ALU.subtract, ALU.mult)
                return ins

            def attention(s, i):
                c = core[s]
                start = KT["tok"] if s == "tok" else Q0
                for step in range(G + 1):
                    if step >= 1:
                        g = step - 1
                        dve.wait_ge(c["neg_turned"], i * G + g + 1)
                        dve.tensor_tensor(QT[:, g, :], start[:, g, :], bank[7][:, (g % 2) * S:(g % 2 + 1) * S],
                                          ALU.add).then_inc(c["queries"], 1)
                    if step < G:
                        g = step
                        for h in range(4 * g, 4 * g + 4):
                            dve.wait_ge(c["scores"], i * H + h + 1)
                            if s == "tok":
                                src, dst = bank[h % 2].rearrange("p (t k) -> p t k", t=T), rowmax[:, :, h]
                            else:
                                src, dst = bank[h % 2][:, 0:3 * P].rearrange("p (b k) -> p b k", b=3), blockmax[:, :, h]
                            dve.tensor_reduce(dst, src, AX_X, ALU.max).then_inc(c["maxed"], 1)
                        dve.wait_ge(c["maxed"], i * H + 4 * g + 4)
                        heads = slice(4 * g, 4 * g + 4)
                        if s == "att":
                            dve.tensor_copy(rowmax[:, 0, heads], blockmax[:, 0, heads])
                            link(dve.tensor_tensor(rowmax[:, 1, heads], blockmax[:, 1, heads],
                                                   blockmax[:, 2, heads], ALU.max))
                        dve.tensor_scalar(negmax[:, :, heads, HD:HD + 1],
                                          rowmax[:, :, heads].rearrange("p t (h a) -> p t h a", a=1),
                                          -1.0, -1.0 if s == "tok" else 0.0, ALU.mult, ALU.add
                                          ).then_inc(c["neg_ready"], 1)
                for t in range(T):
                    dve.wait_ge(c["ctx_turned"], i * T + t + 1)
                    tile = bank[t].rearrange("p (h w) -> p h w", w=32)
                    link(dve.reciprocal(recip[:, t, :], tile[:, :, HD]))
                    dve.tensor_tensor(ctxn[:, t], tile[:, :, 0:HD],
                                      recip[:, t, :].rearrange("p (h a) -> p h a", a=1).to_broadcast([P, H, HD]),
                                      ALU.mult).then_inc(c["ctx_normed"], 1)

            def spread(stat):
                return stat[:].rearrange("p (t a) -> p t a", a=1).to_broadcast([P, T, E])

            with dve.Fori(0, B, 1) as i:
                base[0], base[1] = i, 0
                attention("tok", i)
                dve.wait_ge(attn_out, i + 1)
                for t in range(T):
                    ins = dve.tensor_tensor(resid[:, t, :].rearrange("p (h d) -> p h d", h=H),
                                            bank[3][:, t * D:(t + 1) * D].rearrange("p (h d) -> p h d", h=H),
                                            xpad[:, t, :, 0:HD], ALU.add)
                link(ins)
                normalise(resid).then_inc(x1_normed, 1)
                for pair_of in range(1, NF // 2, 2):
                    dve.wait_ge(up_done, i * (NF // 2) + pair_of + 1)
                    for f in (2 * pair_of, 2 * pair_of + 1):
                        ins = dve.tensor_scalar(hid[:, f, 0:S], bank[UP[pair_of]][:, (f % 2) * S:(f % 2 + 1) * S],
                                                b1_sb[:, f:f + 1], 0.0, ALU.add, ALU.max)
                    ins.then_inc(relu_dve, 1)
                dve.wait_ge(down_done, i + 1)
                dve.wait_ge(x1b_ready, i + 1)
                for t in range(T):
                    ins = dve.tensor_tensor(resid[:, t, :], bank[t][:, 0:D], x1b[:, t, :], ALU.add)
                link(ins)
                normalise(resid).then_inc(y_normed, 1)
                dve.wait_ge(h1_ready, i + 1)
                normalise(h1).then_inc(h1_normed, 1)
                for g in range(G):
                    if g % 2 == 0:
                        dve.wait_ge(q_proj, i * (G // 2) + g // 2 + 1)
                    dve.tensor_scalar(Q0[:, g, :], bank[QB[g // 2]][:, (g % 2) * S:(g % 2 + 1) * S],
                                      bqk[:, 0, g:g + 1], None, ALU.add).then_inc(q_ready, 1)
                dve.wait_ge(v_proj, i + 1)
                for t in range(T):
                    ins = dve.tensor_tensor(vpad[:, t, :, 0:HD],
                                            bank[1][:, t * D:(t + 1) * D].rearrange("p (h d) -> p h d", h=H),
                                            rows[:, 5, :].rearrange("p (h d) -> p h d", h=H), ALU.add)
                ins.then_inc(v_ready, 1)
                attention("att", i)
                dve.wait_ge(core["att"]["ctx_normed"], i * T + T)
                dve.tensor_reduce(zsum[:], ctxn[:].rearrange("p t h d -> p t d h"), AX_X, ALU.add).then_inc(z_ready, 1)
                dve.wait_ge(z_out, i + 1)
                dve.wait_ge(h1b_ready, i + 1)
                dve.wait_ge(out_stored, i * DMA + DMA)
                dve.wait_ge(scattered, i * (T * DMA) + DMA)
                dve.tensor_tensor(h2row[:, :, 0:D], bank[3].rearrange("p (t d) -> p t d", t=T), h1b[:],
                                  ALU.add).then_inc(h2_ready, 1)
                dve.wait_ge(h2_ready, i + 1)
                normalise(h2row).then_inc(h2_normed, 1)
                dve.tensor_copy(h2row[:, :, D + 2], mv[:, :, 0])
                dve.tensor_copy(h2row[:, :, D + 3], rstd[:])
                dve.wait_ge(logits, i + 1)
                link(dve.tensor_copy(lg[:], bank[5][:, 0:T * E].rearrange("p (t e) -> p t e", t=T)))
                link(dve.tensor_reduce(lmax[:], lg[:], AX_X, ALU.max))
                dve.tensor_tensor(lsh[:], lg[:], spread(lmax), ALU.subtract).then_inc(shifted, 1)
                link(dve.tensor_tensor(eq[:], lg[:], spread(lmax), ALU.is_equal))
                link(dve.tensor_tensor(eqr[:], eq[:], rev[:], ALU.mult))
                link(dve.tensor_reduce(first[:], eqr[:], AX_X, ALU.max))
                link(dve.tensor_tensor(onehot[:], eqr[:], spread(first), ALU.is_equal))
                dve.tensor_copy(onehotb[:], onehot[:]).then_inc(onehot_ready, 1)
                dve.wait_ge(exped, i + 1)
                link(dve.tensor_reduce(lsum[:], lexp[:], AX_X, ALU.add))
                dve.reciprocal(h2row[:, :, D], lsum[:])
                dve.wait_ge(ranked, i + 1)
                link(dve.tensor_tensor(posr[:], bank[2][:, 0:T * E].rearrange("p (t e) -> p t e", t=T),
                                       counts[:].rearrange("p (a e) -> p a e", a=1).to_broadcast([P, T, E]), ALU.add))
                dve.tensor_tensor(counts[:], counts[:], bank[2][:, T * E:T * E + E], ALU.add)
                link(dve.tensor_tensor(sel[:], onehot[:], posr[:], ALU.mult))
                link(dve.tensor_reduce(locf[:], sel[:], AX_X, ALU.add))
                dve.tensor_scalar(over[:], locf[:], float(CAP), float(NOWHERE), ALU.is_ge, ALU.mult)
                link(dve.tensor_tensor(sel[:], onehot[:], ebase[:], ALU.mult))
                link(dve.tensor_reduce(slotf[:], sel[:], AX_X, ALU.add))
                link(dve.tensor_tensor(slotf[:], slotf[:], locf[:], ALU.add))
                link(dve.tensor_tensor(slotf[:], slotf[:], over[:], ALU.add))
                dve.tensor_copy(sloti[:], slotf[:]).then_inc(slot_ready, 1)
                assert base[1] == VECTOR_LINKS, base[1]

            with dve.Fori(0, E // 2, 1) as j:
                for k in range(2):
                    e = j * 2 + k
                    dve.wait_ge(e_loaded[k], (j + 1) * (5 * DMA))
                    for t in range(CT):
                        ins = dve.tensor_scalar(xen[:, t, :], xe[:, k, t, 0:D], xe[:, k, t, D + 2:D + 3],
                                                xe[:, k, t, D + 3:D + 4], ALU.subtract, ALU.mult)
                    ins.then_inc(e_normed, 1)
                    dve.wait_ge(e_turned, e + 1)
                    for c in range(C2):
                        ins = dve.tensor_copy(xeT[:, c, :], bank[c])
                    ins.then_inc(eT_ready, 1)
                    for t in range(CT):
                        n = j * (2 * CT) + k * CT + t + 1
                        dve.wait_ge(e_down, n)
                        dve.tensor_tensor(yb[:, t % 2, :], bank[6 + t % 2][:, 0:D], mb2_sb[:, k, :],
                                          ALU.add).then_inc(e_biased, 1)
                        dve.wait_ge(e_biased, n + 1)
                        dve.scalar_tensor_tensor(out=yo[:, k, t, :], in0=yb[:, t % 2, :], scalar=xe[:, k, t, D:D + 1],
                                                 in1=xe[:, k, t, 0:D], op0=ALU.mult, op1=ALU.add).then_inc(e_out, 1)

        @block.tensor
        def _(pe):
            def turn(dst, src, who):
                for c in range(C2):
                    for t in range(T):
                        ins = pe.transpose(dst[:, c * S + t * P:c * S + (t + 1) * P], src(t, c), ident[:])
                ins.then_inc(who, 1)

            def by_feature(tile):
                return lambda t, c: tile[:, t, c * P:(c + 1) * P]

            def attention(s, i):
                c = core[s]
                keys, rounded = KT[s], KH[s]
                qr = rounded if s == "tok" else QH
                values = xpad if s == "tok" else vpad
                causal = s == "att"

                def score(h):
                    g, r = h // 4, 32 * (h % 4)
                    pe.wait_ge(c["keys_rounded"], i * 2 + g // 2 + 1)
                    if causal:
                        pe.wait_ge(q_rounded, i * 2 + g // 2 + 1)
                    if h >= 2:
                        pe.wait_ge(c["maxed"], i * H + h - 1)
                    elif h == 1 and causal:
                        pe.wait_ge(v_ready, i + 1)
                    tile = bank[h % 2]
                    for t, col, n in PRODUCTS[s]:
                        ins = pe.matmul(tile[:, col:col + n], qr[r:r + HD, g, t * P:(t + 1) * P],
                                        rounded[r:r + HD, g, 0:n], start=True, stop=not causal)
                        if causal:
                            d = col + t * P
                            ins = pe.matmul(tile[:, d:d + P], identb[:], maskq[:], start=False, stop=True)
                    ins.then_inc(c["scores"], 1)

                def pair(p):
                    g = p // 2
                    pe.wait_ge(c["queries"], i * G + g + 1)
                    if p == 0:
                        pe.wait_ge(c["keys_rounded"], i * 2 + 2)
                        if causal:
                            pe.wait_ge(q_rounded, i * 2 + 2)
                    if p >= 2:
                        pe.wait_ge(c["probs"], i * (2 * G) + p - 1)
                    for h in (2 * p, 2 * p + 1):
                        r, tile = 32 * (h % 4), bank[2 + h % 4]
                        for kt in range(T):
                            q0 = kt * P if causal else 0
                            col = kt * S
                            ins = pe.matmul(tile[:, col:col + S - q0], keys[r:r + HD + 1, g, kt * P:(kt + 1) * P],
                                            QT[r:r + HD + 1, g, q0:S], start=True, stop=not causal)
                            if causal:
                                ins = pe.matmul(tile[:, col:col + P], identb[:], maskk[:], start=False, stop=True)
                    ins.then_inc(c["scoresT"], 1)

                def product(g):
                    pe.wait_ge(c["probs"], i * (2 * G) + 2 * g + 2)
                    if g >= 1:
                        pe.wait_ge(c["ctx_copied"], i * G + g)
                    for kt in range(T):
                        q0 = kt * P if causal else 0
                        for r in range(4):
                            ins = pe.matmul(bank[6][32 * r:32 * r + 32, (g % 2) * S + q0:(g % 2 + 1) * S],
                                            values[:, kt, 4 * g + r, :],
                                            prob[:, g % 2, r, kt * S:kt * S + S - q0],
                                            start=(kt == 0), stop=(kt == T - 1), skip_group_check=True)
                    ins.then_inc(c["ctx_done"], 1)

                for step in range(G + 2):
                    if 1 <= step <= G:
                        g = step - 1
                        pe.wait_ge(c["neg_ready"], i * G + g + 1)
                        if g >= 1:
                            pe.wait_ge(c["queries"], i * G + g)
                        for t in range(T):
                            ins = pe.transpose(bank[7][:, (g % 2) * S + t * P:(g % 2) * S + (t + 1) * P],
                                               negmax[:, t, 4 * g:4 * g + 4, :].rearrange("p h w -> p (h w)"), ident[:])
                        ins.then_inc(c["neg_turned"], 1)
                    heads = list(range(4 * step, 4 * step + 4)) if step < G else []
                    pairs = [2 * step - 2, 2 * step - 1] if 1 <= step <= G else []
                    for h in heads[:2]:
                        score(h)
                    for n in range(2):
                        if pairs:
                            pair(pairs[n])
                        for h in heads[2 + n:3 + n]:
                            score(h)
                    if step >= 2:
                        product(step - 2)
                pe.wait_ge(c["ctx_copied"], i * G + G)
                for t in range(T):
                    for g in range(G):
                        ins = pe.transpose(bank[t][:, g * P:(g + 1) * P], CU[:, g, t * P:(t + 1) * P], ident[:])
                    ins.then_inc(c["ctx_turned"], 1)

            pe.wait_ge(pool_const, 24)
            pe.wait_ge(ids_cleaned, 1)
            pe.transpose(bank[7][:, 0:NT], ids_f[:], ident[0:NT, 0:NT]).then_inc(ids_turned, 1)
            pe.wait_ge(loaded, N_LOADS * DMA)
            pe.wait_ge(pool_const, 26)
            with pe.Fori(0, B, 1) as i:
                pe.wait_ge(x_padded, i + 1)
                for half in range(2):
                    for g in (2 * half, 2 * half + 1):
                        for t in range(T):
                            ins = pe.transpose(bank[2 + half][:, (g % 2) * S + t * P:(g % 2) * S + (t + 1) * P],
                                               xpad[:, t, 4 * g:4 * g + 4, :].rearrange("p h w -> p (h w)"), ident[:])
                    ins.then_inc(x_turned, 1)
                attention("tok", i)
                pe.wait_ge(core["tok"]["ctx_normed"], i * T + T)
                flat = ctxn[:].rearrange("p t h d -> p t (h d)")
                turn(bank[2], by_feature(flat), ctxn_turned)
                pe.wait_ge(ctxnT_ready, i + 1)
                for t in range(T):
                    for c in range(C2):
                        ins = pe.matmul(bank[3][:, t * D:(t + 1) * D], featT[:, c, t * P:(t + 1) * P], w_o_sb[:, c, :],
                                        start=(c == 0), stop=(c == C2 - 1))
                ins.then_inc(attn_out, 1)
                pe.wait_ge(x1_normed, i + 2)
                turn(bank[4], by_feature(normed), x1_turned)
                pe.wait_ge(x1T_ready, i + 1)
                for f in range(NF):
                    for c in range(C2):
                        ins = pe.matmul(bank[UP[f // 2]][:, (f % 2) * S:(f % 2 + 1) * S],
                                        w1_sb[:, c, f * P:(f + 1) * P], featT[:, c, :],
                                        start=(c == 0), stop=(c == C2 - 1))
                    if f % 2:
                        ins.then_inc(up_done, 1)
                for f in range(NF):
                    pair_of = f // 2
                    if f % 2 == 0:
                        pe.wait_ge(relu_dve if pair_of % 2 else relu_act, i * (NF // 4) + pair_of // 2 + 1)
                    for t in range(T):
                        ins = pe.matmul(bank[t][:, 0:D], hid[:, f, t * P:(t + 1) * P], w2_sb[:, f, :],
                                        start=(f == 0), stop=(f == NF - 1))
                ins.then_inc(down_done, 1)
                pe.wait_ge(h1_normed, i + 1)
                turn(bank[4], by_feature(normed), h1_turned)
                pe.wait_ge(h1T_ready, i + 1)
                for which, banks, ready in ((1, (2, 3), k_proj), (0, QB, q_proj)):
                    for g in range(G):
                        for c in range(C2):
                            ins = pe.matmul(bank[banks[g // 2]][:, (g % 2) * S:(g % 2 + 1) * S],
                                            wqk[:, which, c, 4 * g:4 * g + 4, :].rearrange("p h w -> p (h w)"),
                                            featT[:, c, :], start=(c == 0), stop=(c == C2 - 1))
                        if g % 2:
                            ins.then_inc(ready, 1)
                for t in range(T):
                    for c in range(C2):
                        ins = pe.matmul(bank[1][:, t * D:(t + 1) * D], featT[:, c, t * P:(t + 1) * P], wv_sb[:, c, :],
                                        start=(c == 0), stop=(c == C2 - 1))
                ins.then_inc(v_proj, 1)
                attention("att", i)
                pe.wait_ge(z_ready, i + 1)
                for t in range(T):
                    ins = pe.transpose(bank[2][0:HD, t * P:(t + 1) * P], zsum[:, t, :], ident[:])
                ins.then_inc(z_turned, 1)
                pe.wait_ge(zT_ready, i + 1)
                for t in range(T):
                    ins = pe.matmul(bank[3][:, t * D:(t + 1) * D], zT[:, t * P:(t + 1) * P], wo_sb[:],
                                    start=True, stop=True)
                ins.then_inc(z_out, 1)
                pe.wait_ge(h2_normed, i + 1)
                turn(bank[4], by_feature(normed), h2_turned)
                pe.wait_ge(h2T_ready, i + 1)
                for t in range(T):
                    for c in range(C2):
                        ins = pe.matmul(bank[5][:, t * E:(t + 1) * E], featT[:, c, t * P:(t + 1) * P], wg_sb[:, c, :],
                                        start=(c == 0), stop=(c == C2 - 1))
                ins.then_inc(logits, 1)
                pe.wait_ge(onehot_ready, i + 1)
                pe.matmul(bank[2][:, 0:E], before[:], onehotb[:, 0, :], start=True, stop=True)
                pe.matmul(bank[2][:, E:2 * E], before[:], onehotb[:, 1, :], start=True, stop=False)
                pe.matmul(bank[2][:, E:2 * E], onesb[:], onehotb[:, 0, :], start=False, stop=True)
                pe.matmul(bank[2][:, 2 * E:3 * E], onesb[:], onehotb[:, 0, :], start=True, stop=False)
                pe.matmul(bank[2][:, 2 * E:3 * E], onesb[:], onehotb[:, 1, :], start=False, stop=True
                          ).then_inc(ranked, 1)

            with pe.Fori(0, E // 2, 1) as j:
                for k in range(2):
                    e = j * 2 + k
                    pe.wait_ge(e_normed, e + 1)
                    for c in range(C2):
                        for t in range(CT):
                            ins = pe.transpose(bank[c][:, t * P:(t + 1) * P], xen[:, t, c * P:(c + 1) * P], ident[:])
                    ins.then_inc(e_turned, 1)
                    pe.wait_ge(eT_ready, e + 1)
                    for f in range(NF):
                        if f >= 4:
                            pe.wait_ge(e_relu, j * (2 * NF) + k * NF + f - 3)
                        for c in range(C2):
                            ins = pe.matmul(bank[2 + f % 4], mw1[:, k, c, f * P:(f + 1) * P], xeT[:, c, :],
                                            start=(c == 0), stop=(c == C2 - 1))
                        ins.then_inc(e_up, 1)
                    pe.wait_ge(e_relu, j * (2 * NF) + k * NF + NF)
                    for t in range(CT):
                        if t >= 2:
                            pe.wait_ge(e_biased, j * (2 * CT) + k * CT + t)
                        else:
                            pe.wait_ge(e_biased, j * (2 * CT) + k * CT + 1)
                        for f in range(NF):
                            ins = pe.matmul(bank[6 + t % 2][:, 0:D], hid[:, f, t * P:(t + 1) * P], mw2[:, k, f, :],
                                            start=(f == 0), stop=(f == NF - 1))
                        ins.then_inc(e_down, 1)


_INS = ["x", "L0_tok_emb", "L0_tok_w_o", "L0_tok_w1", "L0_tok_b1", "L0_tok_w2", "L0_tok_b2", "L0_tok_gamma1",
        "L0_tok_beta1", "L0_tok_gamma2", "L0_tok_beta2", "L0_attn_WQ", "L0_attn_bQ", "L0_attn_WK", "L0_attn_bK",
        "L0_attn_WV", "L0_attn_bV", "L0_attn_WO", "L0_attn_bO", "L0_ffn_Wg", "L0_ffn_W1", "L0_ffn_b1",
        "L0_ffn_W2", "L0_ffn_b2"]
_OUTS = [((16, 256, 256), "float32")]


def kernel(**inputs):
    import numpy as _np
    import concourse.bacc as _bacc
    from concourse import mybir as _mybir
    from concourse.bass_utils import run_bass_kernel_spmd as _run

    nc = _bacc.Bacc("TRN2", target_bir_lowering=False, num_devices=1)
    arrays, args = {}, []
    for name in _INS:
        a = _np.ascontiguousarray(inputs[name])
        arrays[f"in_{name}_dram"] = a
        args.append(nc.dram_tensor(f"in_{name}_dram", a.shape, _mybir.dt.from_np(a.dtype), kind="ExternalInput").ap())
    for i, (shape, dtype) in enumerate(_OUTS):
        dt = _mybir.dt.from_np(_np.dtype(dtype))
        args.append(nc.dram_tensor(f"out_{i}_dram", shape, dt, kind="ExternalOutput").ap())
    lm_tower_kernel(nc, *args)
    r = _run(nc, [arrays], core_ids=[0])
    return r.results[0]["out_0_dram"]
```

```python
from contextlib import ExitStack

import concourse.bass as bass
from concourse import mybir

P = 128
ALU = mybir.AluOpType
ACT = mybir.ActivationFunctionType
F32 = mybir.dt.float32
F32R = mybir.dt.float32r
BF16 = mybir.dt.bfloat16
I32 = mybir.dt.int32
AX_X = mybir.AxisListType.X

EPS = 1e-5
MASKED = -400000.0
ROW_EXTRA = 4
DMA = 16
NEWTON = 3

SLOTS = 48
ATT_SLOT = 20
RING = [("S", 0), ("S", 1), ("S", 2), ("S", 3), ("S", 4), ("S", 5), ("M", 0), ("S", 6), ("S", 7), ("S", 8), ("S", 9),
        ("M", 1), ("S", 10), ("S", 11), ("S", 12), ("S", 13), ("M", 2), ("S", 14), ("S", 15), ("M", 3)]
TURNED_SLOT = [7, 8, 9, 10, 12, 13, 14, 15, 17, 18, 19, 20, 21, 22, 23, 24]
VALUE_SLOT = [11, 16, 21, 26]
ATT_BANK, ATT_LEFT = [7, 5, 6, 7, 5, 6, 7, 5], [0, 0, 0, 1, 2, 3, 4, 5]
TOK_BANK, TOK_LEFT = [7, 6, 7, 7, 7, 6, 7, 5], [0, 0, 1, 3, 4, 2, 5, 0]
ATT_TURN_SLOT = [17, 18, 19, 20, 21, 22, 23, 24]
TOK_TURN_SLOT = [33, 35, 37, 41, 43, 45, 46, 47]
DOWN_SLOT = [0, 1, 3, 4]
UP = [(38, 6), (40, 5), (42, 6), (44, 5)]
STEADY_VECTOR = 80
STEADY_POOL = 4


def lm_tower_kernel(nc, x, emb, w_o, w1, b1, w2, b2, gamma1, beta1, gamma2, beta2,
                    WQ, bQ, WK, bK, WV, bV, WO, bO, Wg, mW1, mb1, mW2, mb2, out):
    B, S = x.shape
    V, D = emb.shape
    F = w1.shape[1]
    E, _, MF = mW1.shape
    HD = WO.shape[0]
    H = D // HD
    T = S // P
    C2 = D // P
    NF = F // P
    N = B * S
    CAP = -(-N // E)
    CT = CAP // P
    G = H // 4
    NB = H // 2
    ROW = D + ROW_EXTRA
    NT = N // P
    NR = len(RING)
    assert (T, C2, NF, HD, CT, G) == (2, 2, 8, 16, 4, 4) and MF == F and B >= 4
    NOWHERE = 1 << 20
    SCALE = float(HD) ** -0.5

    slots_dram = nc.dram_tensor("expert_slots", [E * CAP, ROW], F32).ap()

    with ExitStack() as ctx:
        def sb(name, shape, dt=F32):
            return ctx.enter_context(nc.sbuf_tensor(name, shape, dt))

        def sem(name):
            return ctx.enter_context(nc.semaphore(name))

        bank = [ctx.enter_context(nc.psum_tensor(f"bank{k}", [P, 512], F32))[:] for k in range(8)]

        ident = sb("ident", [P, P])
        identr = sb("identr", [P, P], F32R)
        identb = sb("identb", [P, P], BF16)
        maskq = sb("maskq", [P, P], BF16)
        maskk = sb("maskk", [P, P], BF16)
        before = sb("before", [P, P], BF16)
        onesb = sb("onesb", [P, P], BF16)
        zerob = sb("zerob", [P, P], BF16)
        half_rows = sb("half_rows", [P, 4])
        headmask = sb("headmask", [P, 2])
        w_o_sb = sb("w_o_sb", [P, C2, D])
        w1_sb = sb("w1_sb", [P, C2, F])
        w2_sb = sb("w2_sb", [P, NF, D])
        wq_sb = sb("wq_sb", [P, C2, D])
        wk_sb = sb("wk_sb", [P, C2, D])
        wv_sb = sb("wv_sb", [P, C2, D])
        wg_sb = sb("wg_sb", [P, C2, E])
        wo_sb = sb("wo_sb", [HD, D])
        b1_sb = sb("b1_sb", [P, NF])
        g1c = sb("g1c", [P, C2])
        be1c = sb("be1c", [P, C2])
        ROWS = dict(gamma1=0, beta1=1, b2=2, gamma2=3, beta2=4, bV=5, bO=6, bQ=7, bK=8)
        rows = sb("rows", [P, len(ROWS), D])
        be1b2 = sb("be1b2", [P, D])
        bo16 = sb("bo16", [P, D])
        ids_i = sb("ids_i", [NT, P], I32)
        ids_f = sb("ids_f", [NT, P])
        ids_n = sb("ids_n", [NT, P])
        idx_all = sb("idx_all", [P, NT + T], I32)
        ebase = sb("ebase", [P, T, E])
        rev = sb("rev", [P, T, E])
        empty = sb("empty", [P, ROW])

        gidx = sb("gidx", [P, T], I32)
        xg = sb("xg", [P, T, D])
        values = {s: sb(f"values_{s}", [P, T, H, 32]) for s in ("tok", "att")}
        xq_parts = sb("xq_parts", [P, T, NB, 5, 2 * HD], F32R)
        k_parts = sb("k_parts", [P, T, NB, 4, 2 * HD], F32R)
        unsplit = sb("unsplit", [P, T, D])
        QS = {s: sb(f"QS_{s}", [P, NB, S], F32R) for s in ("tok", "att")}
        KS = {s: sb(f"KS_{s}", [P, NB, 2, S], F32R) for s in ("tok", "att")}
        blockmax = sb("blockmax", [P, 3, H])
        negmax = sb("negmax", [P, T, H])
        negmaxT = sb("negmaxT", [P, G, S], F32R)
        prob = sb("prob", [P, 2, 4, 512])
        CU = sb("CU", [P, G, S])
        recip = sb("recip", [P, T, H])
        ctxn = sb("ctxn", [P, T, H, HD])
        feats = sb("feats", [P, 4, C2, S])
        ctxnT, x1T, h1T, h2T = (feats[:, k] for k in range(4))
        hid = sb("hid", [P, NF, CAP])
        resid = sb("resid", [P, T, D])
        normed = sb("normed", [P, T, D])
        normed_h1 = sb("normed_h1", [P, T, D])
        normed_h2 = sb("normed_h2", [P, T, D])
        scaled = sb("scaled", [P, T, D])
        x1b = sb("x1b", [P, T, D])
        h1 = sb("h1", [P, T, D])
        h1b = sb("h1b", [P, T, D])
        NORMS = ("x1", "y", "h1", "h2")
        stats = sb("stats", [P, T, 6])
        mv = {k: sb(f"mv_{k}", [P, T, 2]) for k in NORMS}
        rstd = {k: sb(f"rstd_{k}", [P, T]) for k in NORMS}
        shift = {k: sb(f"shift_{k}", [P, T]) for k in NORMS}
        var = sb("var", [P, T])
        halved = sb("halved", [P, T], I32)
        corr = sb("corr", [P, T])
        zsum = sb("zsum", [P, T, HD])
        zT = sb("zT", [HD, S])
        h2row = sb("h2row", [P, T, ROW])
        tokid = sb("tokid", [P, T], I32)
        lg = sb("lg", [P, T, E])
        lmax = sb("lmax", [P, T])
        lsh = sb("lsh", [P, T, E])
        lexp = sb("lexp", [P, T, E])
        lsum = sb("lsum", [P, T])
        eq = sb("eq", [P, T, E])
        eqr = sb("eqr", [P, T, E])
        first = sb("first", [P, T])
        onehot = sb("onehot", [P, T, E])
        onehotb = sb("onehotb", [P, T, E], BF16)
        posr = sb("posr", [P, T, E])
        sel = sb("sel", [P, T, E])
        locf = sb("locf", [P, T])
        slotf = sb("slotf", [P, T])
        over = sb("over", [P, T])
        sloti = sb("sloti", [P, T], I32)
        counts = sb("counts", [P, E])
        xe = sb("xe", [P, 2, CT, ROW])
        xen = CU[:]
        xeT = values["tok"][:].rearrange("p t h w -> p (t h w)").rearrange("p (c n) -> p c n", c=C2)
        mw1 = [w1_sb, feats[:].rearrange("p k c s -> p (k c s)").rearrange("p (c f) -> p c f", c=C2)]
        mw2 = [w2_sb, sb("mw2", [P, NF, D])]
        mb1_sb = sb("mb1_sb", [P, 2, NF])
        mb2_sb, yb = scaled, unsplit
        yo = prob[:, :, :, 0:D]

        loaded = sem("loaded")
        ids_loaded = sem("ids_loaded")
        pool_const = sem("pool_const")
        vec_const = sem("vec_const")
        ids_cleaned = sem("ids_cleaned")
        ids_turned = sem("ids_turned")
        ids_ready = sem("ids_ready")
        vector_step = sem("vector_step")
        pool_step = sem("pool_step")
        ring_filled = sem("ring_filled")
        ring_read = sem("ring_read")
        neg_ready = sem("neg_ready")
        scores = sem("scores")
        probs = sem("probs")
        ctx_done = sem("ctx_done")
        ctx_copied = sem("ctx_copied")
        ctx_turned = {s: sem(f"ctx_turned_{s}") for s in ("tok", "att")}
        ctx_normed = {s: sem(f"ctx_normed_{s}") for s in ("tok", "att")}
        turned = {s: sem(f"turned_{s}") for s in ("tok", "att")}
        stacked = {s: sem(f"stacked_{s}") for s in ("tok", "att")}
        values_ready = {s: sem(f"values_ready_{s}") for s in ("tok", "att")}
        gathered = sem("gathered")
        x_split, x_parts = sem("x_split"), sem("x_parts")
        ctxnT_turned = sem("ctxnT_turned")
        ctxnT_ready = sem("ctxnT_ready")
        attn_out = sem("attn_out")
        x_added = sem("x_added")
        x1_stats = sem("x1_stats")
        x1_normed = sem("x1_normed")
        x1_turned = sem("x1_turned")
        x1T_ready = sem("x1T_ready")
        x1b_ready = sem("x1b_ready")
        up_done = sem("up_done")
        relu_act = sem("relu_act")
        relu_dve = sem("relu_dve")
        down_done = sem("down_done")
        y_added = sem("y_added")
        y_stats = sem("y_stats")
        y_normed = sem("y_normed")
        h1_ready = sem("h1_ready")
        h1_stats = sem("h1_stats")
        h1_normed = sem("h1_normed")
        h1_turned = sem("h1_turned")
        h1T_ready = sem("h1T_ready")
        h1b_ready = sem("h1b_ready")
        q_proj, k_proj, v_proj = sem("q_proj"), sem("k_proj"), sem("v_proj")
        q_ready, k_ready = sem("q_ready"), sem("k_ready")
        q_split, k_split = sem("q_split"), sem("k_split")
        q_parted, k_parted = sem("q_parted"), sem("k_parted")
        z_ready = sem("z_ready")
        z_turned = sem("z_turned")
        zT_ready = sem("zT_ready")
        z_out = sem("z_out")
        h2_ready = sem("h2_ready")
        h2_stats = sem("h2_stats")
        h2_normed = sem("h2_normed")
        h2_turned = sem("h2_turned")
        h2T_ready = sem("h2T_ready")
        logits = sem("logits")
        logits_read = sem("logits_read")
        shifted = sem("shifted")
        exped = sem("exped")
        onehot_ready = sem("onehot_ready")
        ranked = sem("ranked")
        ranks_read = sem("ranks_read")
        slot_ready = sem("slot_ready")
        tokid_ready = sem("tokid_ready")
        out_stored = sem("out_stored")
        scattered = sem("scattered")
        e_loaded = [sem("e_loaded0"), sem("e_loaded1")]
        e_normed = sem("e_normed")
        e_turned = sem("e_turned")
        eT_ready = sem("eT_ready")
        e_up = sem("e_up")
        e_relu = sem("e_relu")
        e_down = sem("e_down")
        e_biased = sem("e_biased")
        e_out = sem("e_out")
        e_scattered = [sem("e_scattered0"), sem("e_scattered1")]

        out_rows = out.rearrange("b (t p) d -> p b t d", p=P).rearrange("p b t d -> p (b t) d")
        flat_out = out.rearrange("b s d -> (b s) d")

        passed = sem("passed")

        def after(eng, semaphore, value):
            if not isinstance(value, int) or value > 0:
                eng.wait_ge(semaphore, value)

        def after_apart(eng, semaphore, value):
            if not isinstance(value, int) or value > 0:
                eng.wait_ge(semaphore, value)
                eng.sem_inc(passed, 1)

        def count(i, lag, per, c):
            return i * per + (c - lag * per)

        def run_count(s, i, per, c):
            if isinstance(i, int) and i in (0, B):
                return (2 * i - (i == B)) * per + c
            return i * (2 * per) + ((-1 if s == "tok" else 0) * per + c)

        def first_run(i, per, c):
            return run_count("att" if isinstance(i, int) and i == B else "tok", i, per, c)

        def active(i, steady):
            return (True, True, True) if steady else (i < B, 1 <= i <= B, 2 <= i)

        def iterations(eng, body):
            for i in (0, 1):
                body(i, active(i, False))
            with eng.Fori(2, B, 1) as i:
                body(i, active(i, True))
            for i in (B, B + 1):
                body(i, active(i, False))

        block = ctx.enter_context(nc.Block())

        N_LOADS = 20

        @block.sync
        def _(sp):
            sp.dma_start(ids_i[:], x.rearrange("b (t p) -> (b t) p", p=P)).then_inc(ids_loaded, DMA)

            def load(dst, src):
                sp.dma_start(dst, src).then_inc(loaded, DMA)

            with nc.allow_non_contiguous_dma(reason="a few bias columns"):
                load(b1_sb[:], b1.rearrange("(f p) -> p f", p=P))
                load(g1c[:], gamma1.rearrange("(c p) -> p c", p=P))
                load(be1c[:], beta1.rearrange("(c p) -> p c", p=P))
            for k, r in enumerate((gamma1, beta1, b2, gamma2, beta2, bV, bO, bQ, bK)):
                load(rows[:, k, :], r.rearrange("(a d) -> a d", a=1).to_broadcast([P, D]))
            load(w_o_sb[:], w_o.rearrange("(c p) n -> p c n", p=P))
            load(w1_sb[:], w1.rearrange("(c p) n -> p c n", p=P))
            load(w2_sb[:], w2.rearrange("(c p) n -> p c n", p=P))
            load(wq_sb[:], WQ.rearrange("(c p) n -> p c n", p=P))
            load(wk_sb[:], WK.rearrange("(c p) n -> p c n", p=P))
            load(wv_sb[:], WV.rearrange("(c p) n -> p c n", p=P))
            load(wo_sb[:], WO)
            load(wg_sb[:], Wg.rearrange("(c p) n -> p c n", p=P))

            sp.sem_inc(out_stored, DMA)

            def iteration(i, on):
                if on[2]:
                    after(sp, h2_ready, count(i, 2, 1, 1))
                    sp.dma_start(out_rows[:, bass.ds(count(i, 2, T, 0), T), :], h2row[:, :, 0:D]).then_inc(out_stored, DMA)

            iterations(sp, iteration)

            def load_expert(e, k):
                w = e_loaded[k]
                sp.dma_start(xe[:, k], slots_dram.rearrange("(e t p) r -> e p t r", t=CT, p=P)[e]).then_inc(w, DMA)
                sp.dma_start(mw1[k][:], mW1.rearrange("e (c p) f -> e p c f", p=P)[e]).then_inc(w, DMA)
                sp.dma_start(mw2[k][:], mW2.rearrange("e (c p) f -> e p c f", p=P)[e]).then_inc(w, DMA)
                with nc.allow_non_contiguous_dma(reason="bias columns"):
                    sp.dma_start(mb1_sb[:, k], mb1.rearrange("e (f p) -> e p f", p=P)[e]).then_inc(w, DMA)
                sp.dma_start(mb2_sb[:, k], mb2.rearrange("e (a d) -> e a d", a=1)[e].to_broadcast([P, D])).then_inc(w, DMA)

            sp.wait_ge(scattered, DMA * T * B + DMA)
            load_expert(0, 0)
            load_expert(1, 1)
            with sp.Fori(0, E // 2 - 1, 1) as j:
                for k in range(2):
                    sp.wait_ge(e_scattered[k], (j + 1) * (CT * DMA))
                    load_expert(2 * j + 2 + k, k)

        @block.gpsimd
        def _(pool):
            pool.memset(empty[:], 0.0).then_inc(pool_const, 1)
            pool.wait_ge(pool_const, 1)
            pool.memset(empty[:].bitcast(I32)[:, D + 1:D + 2], NOWHERE).then_inc(pool_const, 1)
            pool.memset(ident[:], 0.0).then_inc(pool_const, 1)
            pool.memset(idx_all[:], 0).then_inc(pool_const, 1)
            pool.memset(onesb[:], 1.0).then_inc(pool_const, 1)
            pool.memset(zerob[:], 0.0).then_inc(pool_const, 1)
            pool.memset(half_rows[:], 1.0).then_inc(pool_const, 1)
            pool.memset(CU[:], 0.0).then_inc(pool_const, 1)
            pool.memset(values["tok"][:], 0.0).then_inc(pool_const, 1)
            pool.memset(values["att"][:], 0.0).then_inc(pool_const, 1)
            pool.memset(counts[:], 0.0).then_inc(pool_const, 1)
            pool.wait_ge(pool_const, 11)
            for s in ("tok", "att"):
                pool.memset(values[s][:, :, :, HD:HD + 1], 1.0).then_inc(pool_const, 1)
            pool.affine_select(out=ident[:], in_=ident[:], compare_op=ALU.not_equal, fill=1.0, base=0,
                               pattern=[[-1, P]], channel_multiplier=1).then_inc(pool_const, 1)
            pool.affine_select(out=maskq[:], in_=zerob[:], compare_op=ALU.is_ge, fill=MASKED, base=0,
                               pattern=[[-1, P]], channel_multiplier=1).then_inc(pool_const, 1)
            pool.affine_select(out=maskk[:], in_=zerob[:], compare_op=ALU.is_ge, fill=MASKED, base=0,
                               pattern=[[1, P]], channel_multiplier=-1).then_inc(pool_const, 1)
            pool.affine_select(out=before[:], in_=onesb[:], compare_op=ALU.is_gt, fill=0.0, base=0,
                               pattern=[[1, P]], channel_multiplier=-1).then_inc(pool_const, 1)
            pool.affine_select(out=half_rows[:], in_=half_rows[:], compare_op=ALU.is_ge, fill=0.0, base=0,
                               pattern=[[-32, 4]], channel_multiplier=1).then_inc(pool_const, 1)
            pool.wait_ge(pool_const, 18)
            pool.affine_select(out=half_rows[:], in_=half_rows[:], compare_op=ALU.is_ge, fill=0.0, base=HD - 1,
                               pattern=[[32, 4]], channel_multiplier=-1).then_inc(pool_const, 1)
            pool.iota(tokid[:], pattern=[[P, T]], base=-S, channel_multiplier=1).then_inc(pool_const, 1)
            pool.iota(ebase[:], pattern=[[0, T], [CAP, E]], base=0, channel_multiplier=0,
                      allow_small_or_imprecise_dtypes=True).then_inc(pool_const, 1)
            pool.iota(rev[:], pattern=[[0, T], [-1, E]], base=E, channel_multiplier=0,
                      allow_small_or_imprecise_dtypes=True).then_inc(pool_const, 1)
            pool.tensor_copy(identb[:], ident[:]).then_inc(pool_const, 1)

            steps = [0, 0]

            def link(ins, i):
                ins.then_inc(pool_step, 1)
                steps[1] += 1
                after_apart(pool, pool_step, i * steps[0] + steps[1])

            def gather(i, now):
                link(pool.tensor_copy(gidx[:], idx_all[:, bass.ds(i * T, T)]), now)
                for t in range(T):
                    pool.indirect_dma_start(xg[:, t, :], None, emb, bass.IndirectOffsetOnAxis(gidx[:, t:t + 1], 0)
                                            ).then_inc(gathered, DMA)

            def take_values(i):
                after_apart(pool, gathered, count(i, 0, T * DMA, T * DMA))
                pool.tensor_copy(values["tok"][:, :, :, 0:HD],
                                 xg[:].rearrange("p t (h d) -> p t h d", h=H)).then_inc(values_ready["tok"], 1)

            pool.wait_ge(ids_ready, 1)
            gather(0, 0)
            take_values(0)
            pool.dma_start(slots_dram.rearrange("(p s) r -> p s r", p=P),
                           empty[:].rearrange("p (a r) -> p a r", a=1).to_broadcast([P, E * CAP // P, ROW])
                           ).then_inc(scattered, DMA)
            pool.wait_ge(loaded, N_LOADS * DMA)
            pool.wait_ge(vec_const, 10)
            pool.wait_ge(scattered, DMA)

            def iteration(i, on):
                tok, att, routed = on
                at_start = steps[1]
                if tok:
                    after_apart(pool, values_ready["tok"], count(i, 0, 1, 1))
                    after_apart(pool, x_split, count(i, 0, 1, 1))
                    gather(i + 1, i)
                if att:
                    after_apart(pool, x1b_ready, count(i, 1, 1, 1))
                    after_apart(pool, y_normed, count(i, 1, 1, 1))
                    for t in range(T):
                        ins = pool.tensor_tensor(scaled[:, t, :], normed[:, t, :], rows[:, ROWS["gamma2"], :], ALU.mult)
                    link(ins, i)
                    for t in range(T):
                        ins = pool.tensor_tensor(h1[:, t, :], scaled[:, t, :], rows[:, ROWS["beta2"], :], ALU.add)
                    ins.then_inc(h1_ready, 1)
                    if routed:
                        after_apart(pool, h2_ready, count(i, 2, 1, 1))
                    after_apart(pool, h1_ready, count(i, 1, 1, 1))
                    for t in range(T):
                        ins = pool.tensor_tensor(h1b[:, t, :], h1[:, t, :], bo16[:], ALU.add)
                    ins.then_inc(h1b_ready, 1)
                if tok:
                    after_apart(pool, x_added, count(i, 0, 1, 1))
                    take_values(i + 1)
                    after_apart(pool, x1_normed, count(i, 0, 1, 1))
                    for t in range(T):
                        ins = pool.tensor_tensor(scaled[:, t, :], normed[:, t, :], rows[:, ROWS["gamma1"], :], ALU.mult)
                    link(ins, i)
                    for t in range(T):
                        ins = pool.tensor_tensor(x1b[:, t, :], scaled[:, t, :], be1b2[:], ALU.add)
                    ins.then_inc(x1b_ready, 1)
                if routed:
                    link(pool.tensor_scalar(tokid[:], tokid[:], float(S), None, ALU.add), i)
                    after_apart(pool, scattered, count(i, 2, T * DMA, DMA))
                    pool.tensor_copy(h2row[:, :, D + 1:D + 2].bitcast(I32),
                                     tokid[:].rearrange("p (t a) -> p t a", a=1)).then_inc(tokid_ready, 1)
                    after_apart(pool, slot_ready, count(i, 2, 1, 1))
                    after_apart(pool, tokid_ready, count(i, 2, 1, 1))
                    for t in range(T):
                        pool.indirect_dma_start(slots_dram, bass.IndirectOffsetOnAxis(sloti[:, t:t + 1], 0),
                                                h2row[:, t, :], None, bounds_check=E * CAP - 1,
                                                oob_is_err=False).then_inc(scattered, DMA)
                return steps[1] - at_start

            def pooled(i, on):
                if isinstance(i, int):
                    if i == B and steps[0]:
                        steps[0], steps[1] = 0, steps[1] + (B - 2) * STEADY_POOL
                    iteration(i, on)
                else:
                    steps[0], steps[1] = STEADY_POOL, steps[1] - 2 * STEADY_POOL
                    assert iteration(i, on) == STEADY_POOL
                    steps[1] += STEADY_POOL

            iterations(pool, pooled)

            pool.wait_ge(out_stored, B * DMA + DMA)
            with pool.Fori(0, E // 2, 1) as j:
                for k in range(2):
                    for t in range(CT):
                        after_apart(pool, e_out, j * (2 * CT) + k * CT + t + 1)
                        pool.indirect_dma_start(flat_out, bass.IndirectOffsetOnAxis(
                            xe[:, k, t, D + 1:D + 2].bitcast(I32), 0), yo[:, k, t, :], None,
                            bounds_check=N - 1, oob_is_err=False).then_inc(e_scattered[k], DMA)
            pool.wait_ge(gathered, (B + 1) * T * DMA)
            for k in range(2):
                pool.wait_ge(e_scattered[k], E // 2 * CT * DMA)

        @block.scalar
        def _(act):
            def core(s, i, n):
                if n in TURNED_SLOT:
                    h = TURNED_SLOT.index(n)
                    g, r = h // 4, h % 4
                    after(act, scores, run_count(s, i, H, h + 1))
                    after(act, ctx_done, run_count(s, i, G, g - 1))
                    a = 0 if s == "tok" else P
                    act.activation(prob[:, g % 2, r, a:], bank[2 + h % 2][:, a:], ACT.Exp,
                                   scale=SCALE).then_inc(probs, 1)
                if n in VALUE_SLOT:
                    g = VALUE_SLOT.index(n)
                    after(act, ctx_done, run_count(s, i, G, g + 1))
                    if g == 0:
                        if s == "tok":
                            after(act, ctx_turned["att"], count(i, 2, T, T))
                        elif i < B if isinstance(i, int) else True:
                            after(act, ctx_turned["tok"], count(i, 0, T, T))
                    act.activation(CU[:, g, :], bank[4][:, 0:S], ACT.Copy).then_inc(ctx_copied, 1)

            def stack(s, i, m, k):
                after(act, turned[s], count(i, 0, 2 * G, m + 1))
                b = 2 * (m // 2)
                src = bank[k].rearrange("p (b q) -> p b q", b=2)
                if m % 2:
                    act.activation(QS[s][:, b:b + 2, :], src, ACT.Copy).then_inc(stacked[s], 1)
                else:
                    for r in range(2):
                        ins = act.activation(KS[s][:, b:b + 2, r, :], src, ACT.Copy, scale=headmask[:, r:r + 1])
                    ins.then_inc(stacked[s], 1)

            def apply(k, dst, src):
                for t in range(T):
                    ins = act.activation(dst[:, t, :], src[:, t, :], ACT.Identity,
                                         bias=shift[k][:, t:t + 1], scale=rstd[k][:, t:t + 1])
                return ins

            def leave(dst, k):
                return act.activation(dst, bank[k].rearrange("p (c q) -> p c q", c=C2), ACT.Copy)

            def relu(i, pair_of, k):
                after(act, up_done, count(i, 0, NF // 2, pair_of + 1))
                for f in (2 * pair_of, 2 * pair_of + 1):
                    ins = act.activation(hid[:, f, 0:S], bank[k][:, (f % 2) * S:(f % 2 + 1) * S],
                                         ACT.Relu, bias=b1_sb[:, f:f + 1])
                ins.then_inc(relu_act, 1)

            def repeat(parts, places, who):
                flat = parts[:].rearrange("p t b l w -> p (t b) l w")
                for src, dst in places:
                    ins = act.activation(flat[:, :, dst, :], flat[:, :, src, :], ACT.Copy)
                ins.then_inc(who, 1)

            act.wait_ge(vec_const, 10)
            act.wait_ge(x_split, 1)
            repeat(xq_parts, ((1, 4), (2, 3), (1, 0)), x_parts)
            for m in range(2 * G):
                stack("tok", 0, m, TOK_BANK[m])
            act.wait_ge(loaded, N_LOADS * DMA)

            def iteration(i, on):
                tok, att, routed = on
                for n in range(SLOTS):
                    if tok:
                        core("tok", i, n)
                    if att:
                        core("att", i, n - ATT_SLOT)
                    if n == 7 and att:
                        after(act, y_stats, count(i, 1, 1, 1))
                        after(act, x1b_ready, count(i, 1, 1, 1))
                        apply("y", normed, resid).then_inc(y_normed, 1)
                    if n == 12 and att:
                        after(act, h1_stats, count(i, 1, 1, 1))
                        apply("h1", normed_h1, h1).then_inc(h1_normed, 1)
                    if n == 13 and att:
                        after(act, h1_turned, count(i, 1, 1, 1))
                        leave(h1T, 6).then_inc(h1T_ready, 1)
                    if n == 15 and att:
                        after(act, q_split, count(i, 1, 1, 1))
                        repeat(xq_parts, ((1, 0), (2, 3)), q_parted)
                    if n == 16 and att:
                        after(act, k_split, count(i, 1, 1, 1))
                        repeat(k_parts, ((1, 2), (0, 3)), k_parted)
                    if n in ATT_TURN_SLOT and att:
                        m = ATT_TURN_SLOT.index(n)
                        stack("att", i - 1, m, ATT_BANK[m])
                    if n == 26 and routed:
                        after(act, z_turned, count(i, 2, 1, 1))
                        act.activation(zT[:], bank[6][0:HD, 0:S], ACT.Copy).then_inc(zT_ready, 1)
                    if n == 30 and tok:
                        after(act, ctxnT_turned, count(i, 0, 1, 1))
                        leave(ctxnT, 7).then_inc(ctxnT_ready, 1)
                    if n == 31 and routed:
                        after(act, h2_stats, count(i, 2, 1, 1))
                        apply("h2", normed_h2, h2row[:, :, 0:D]).then_inc(h2_normed, 1)
                    if n == 32 and tok:
                        after(act, x_split, count(i, 0, 1, 2))
                        repeat(xq_parts, ((1, 4), (2, 3), (1, 0)), x_parts)
                    if n == 32 and routed:
                        after(act, h2_turned, count(i, 2, 1, 1))
                        leave(h2T, 6).then_inc(h2T_ready, 1)
                    if n == 34 and tok:
                        after(act, x1_stats, count(i, 0, 1, 1))
                        after(act, h1_ready, i)
                        apply("x1", normed, resid).then_inc(x1_normed, 1)
                    if n == 36 and routed:
                        after(act, shifted, count(i, 2, 1, 1))
                        act.activation(lexp[:], lsh[:], ACT.Exp).then_inc(exped, 1)
                    if n == 36 and tok:
                        after(act, x1_turned, count(i, 0, 1, 1))
                        for c in range(C2):
                            ins = act.activation(x1T[:, c, :], bank[5][:, c * S:(c + 1) * S], ACT.Identity,
                                                 bias=be1c[:, c:c + 1], scale=g1c[:, c:c + 1])
                        ins.then_inc(x1T_ready, 1)
                    for pair_of in (0, 2):
                        if n == UP[pair_of][0] + 1 and tok:
                            relu(i, pair_of, UP[pair_of][1])
                    if n in TOK_TURN_SLOT and tok:
                        m = TOK_TURN_SLOT.index(n)
                        stack("tok", i + 1, m, TOK_BANK[m])

            iterations(act, iteration)

            with act.Fori(0, E // 2, 1) as j:
                for k in range(2):
                    for f in range(NF):
                        act.wait_ge(e_up, j * (2 * NF) + k * NF + f + 1)
                        act.activation(hid[:, f, :], bank[2 + f % 4], ACT.Relu,
                                       bias=mb1_sb[:, k, f:f + 1]).then_inc(e_relu, 1)

        @block.vector
        def _(dve):
            done = [0]

            def const(ins):
                ins.then_inc(vec_const, 1)
                done[0] += 1
                dve.wait_ge(vec_const, done[0])

            dve.sem_inc(e_biased, 1)
            dve.wait_ge(pool_const, 23)
            const(dve.tensor_reduce(headmask[:, 0:1], half_rows[:], AX_X, ALU.add))
            const(dve.tensor_scalar(headmask[:, 1:2], headmask[:, 0:1], -1.0, 1.0, ALU.mult, ALU.add))
            const(dve.tensor_copy(identr[:], ident[:]))
            const(dve.tensor_copy(negmaxT[:], CU[:]))
            dve.wait_ge(ids_loaded, DMA)
            const(dve.tensor_copy(ids_f[:], ids_i[:]))
            const(dve.tensor_scalar(ids_n[:], ids_f[:], 0.0, float(V), ALU.is_lt, ALU.mult))
            const(dve.tensor_tensor(ids_f[:], ids_f[:], ids_n[:], ALU.add))
            const(dve.tensor_scalar(ids_f[:], ids_f[:], float(V - 1), 0.0, ALU.min, ALU.max))
            dve.sem_inc(ids_cleaned, 1)
            dve.wait_ge(ids_turned, 1)
            dve.tensor_copy(idx_all[:, 0:NT], bank[7][:, 0:NT]).then_inc(ids_ready, 1)
            dve.wait_ge(loaded, N_LOADS * DMA)
            const(dve.tensor_tensor(be1b2[:], rows[:, ROWS["beta1"], :], rows[:, ROWS["b2"], :], ALU.add))
            const(dve.tensor_scalar(bo16[:], rows[:, ROWS["bO"], :], float(H), None, ALU.mult))

            links = [None, 0, 0]

            def link(ins, apart=False):
                ins.then_inc(vector_step, 1)
                links[2] += 1
                (after_apart if apart else after)(dve, vector_step, links[0] * links[1] + links[2])

            def newton(k):
                link(dve.scalar_tensor_tensor(out=corr[:], in0=rstd[k][:], scalar=-0.5, in1=rstd[k][:],
                                              op0=ALU.mult, op1=ALU.mult))
                link(dve.tensor_tensor(corr[:], corr[:], var[:], ALU.mult))
                link(dve.scalar_tensor_tensor(out=rstd[k][:], in0=corr[:], scalar=1.5, in1=rstd[k][:],
                                              op0=ALU.add, op1=ALU.mult))

            def moments(k, src):
                for t in range(T):
                    ins = dve.bn_stats(stats[:, t, :], src[:, t, 0:D])
                link(ins, apart=True)
                for t in range(T):
                    ins = dve.bn_aggr(mv[k][:, t, :], stats[:, t, :])
                link(ins)
                link(dve.tensor_scalar(var[:], mv[k][:, :, 1], EPS, None, ALU.add))
                link(dve.tensor_scalar(halved[:], var[:].bitcast(I32), 1, None, ALU.logical_shift_right))
                link(dve.tensor_scalar(rstd[k][:].bitcast(I32), halved[:], -1.0, float(0x5F3759DF), ALU.mult, ALU.add))

            def deviation(k):
                for _ in range(NEWTON):
                    newton(k)
                return dve.scalar_tensor_tensor(out=shift[k][:], in0=mv[k][:, :, 0], scalar=-1.0, in1=rstd[k][:],
                                                op0=ALU.mult, op1=ALU.mult)

            def core(s, i, n):
                if not 0 <= n < NR:
                    return
                kind, index = RING[n]
                filled = run_count(s, i, NR, n + 1)
                after(dve, ring_filled, filled)
                if kind == "M":
                    dve.tensor_copy(negmaxT[0:4, index, :], bank[n % 2][0:4, 0:S]).then_inc(ring_read, 1)
                    return
                h = index
                if s == "tok":
                    src, dst = bank[n % 2].rearrange("p (t k) -> p t k", t=T), blockmax[:, 0:T, h]
                else:
                    src, dst = bank[n % 2][:, 0:3 * P].rearrange("p (b k) -> p b k", b=3), blockmax[:, :, h]
                dve.tensor_reduce(dst, src, AX_X, ALU.max).then_inc(ring_read, 1)
                if h % 4 == 3:
                    after(dve, ring_read, filled)
                    heads = slice(h - 3, h + 1)
                    if s == "att":
                        link(dve.tensor_tensor(blockmax[:, 1, heads], blockmax[:, 1, heads],
                                               blockmax[:, 2, heads], ALU.max))
                    dve.tensor_scalar(negmax[:, :, heads], blockmax[:, 0:T, heads], -1.0, None,
                                      ALU.mult).then_inc(neg_ready, 1)

            def normalise_ctx(s, i, lag, banks):
                for t in range(T):
                    after(dve, ctx_turned[s], count(i, lag, T, t + 1))
                    tile = bank[banks[t]].rearrange("p (h w) -> p h w", w=32)
                    link(dve.reciprocal(recip[:, t, :], tile[:, :, HD]))
                    dve.tensor_tensor(ctxn[:, t], tile[:, :, 0:HD],
                                      recip[:, t, :].rearrange("p (h a) -> p h a", a=1).to_broadcast([P, H, HD]),
                                      ALU.mult).then_inc(ctx_normed[s], 1)

            def split(dst, src, who):
                a = 1 if dst is xq_parts else 0
                flat, src = dst[:].rearrange("p t b l w -> p (t b) l w"), src[:].rearrange("p t (b w) -> p (t b) w", b=NB)
                link(dve.tensor_copy(flat[:, :, a, :], src))
                dve.tensor_tensor(flat[:, :, a + 1, :], src, flat[:, :, a, :].bitcast(F32),
                                  ALU.subtract).then_inc(who, 1)

            def biased(k, bias):
                return (bank[k].rearrange("p (t d) -> p t d", t=T),
                        rows[:, ROWS[bias]:ROWS[bias] + 1, :].to_broadcast([P, T, D]))

            def relu(i, pair_of, k):
                after(dve, up_done, count(i, 0, NF // 2, pair_of + 1))
                for f in (2 * pair_of, 2 * pair_of + 1):
                    ins = dve.tensor_scalar(hid[:, f, 0:S], bank[k][:, (f % 2) * S:(f % 2 + 1) * S],
                                            b1_sb[:, f:f + 1], 0.0, ALU.add, ALU.max)
                ins.then_inc(relu_dve, 1)

            def spread(stat):
                return stat[:].rearrange("p (t a) -> p t a", a=1).to_broadcast([P, T, E])

            def iteration(i, on):
                tok, att, routed = on
                links[0] = i
                at_start = links[2]
                for n in range(SLOTS):
                    if tok:
                        core("tok", i, n)
                    if att:
                        core("att", i, n - ATT_SLOT)
                    if n == 2 and routed:
                        normalise_ctx("att", i, 2, (5, 6))
                        after(dve, ctx_normed["att"], count(i, 2, T, T))
                        dve.tensor_reduce(zsum[:], ctxn[:].rearrange("p t h d -> p t d h"), AX_X,
                                          ALU.add).then_inc(z_ready, 1)
                    if n == 5 and att:
                        for t in range(T):
                            after(dve, down_done, count(i, 1, T, t + 1))
                            if t == 0:
                                after(dve, x1b_ready, count(i, 1, 1, 1))
                            dve.tensor_tensor(resid[:, t, :], bank[(7, 5)[t]][:, 0:D], x1b[:, t, :], ALU.add
                                              ).then_inc(y_added, 1)
                        after(dve, y_added, count(i, 1, T, T))
                        moments("y", resid)
                    if n == 6 and att:
                        deviation("y").then_inc(y_stats, 1)
                    if n == 10 and att:
                        after(dve, h1_ready, count(i, 1, 1, 1))
                        moments("h1", h1)
                    if n == 11 and att:
                        deviation("h1").then_inc(h1_stats, 1)
                    if n == 14 and att:
                        after(dve, q_proj, count(i, 1, 1, 1))
                        after(dve, turned["tok"], count(i, 0, 2 * G, 2 * G))
                        dve.tensor_tensor(unsplit[:], *biased(7, "bQ"), ALU.add).then_inc(q_ready, 1)
                        after(dve, q_ready, count(i, 1, 1, 1))
                        split(xq_parts, unsplit, q_split)
                    if n == 15 and att:
                        after(dve, k_proj, count(i, 1, 1, 1))
                        after(dve, q_split, count(i, 1, 1, 1))
                        after(dve, turned["att"], count(i, 1, 2 * G, 0))
                        dve.tensor_tensor(unsplit[:], *biased(5, "bK"), ALU.add).then_inc(k_ready, 1)
                        after(dve, k_ready, count(i, 1, 1, 1))
                        split(k_parts, unsplit, k_split)
                    if n == 16 and att:
                        after(dve, v_proj, count(i, 1, 1, 1))
                        after(dve, ctx_done, first_run(i, G, 0))
                        for t in range(T):
                            ins = dve.tensor_tensor(values["att"][:, t, :, 0:HD],
                                                    bank[6][:, t * D:(t + 1) * D].rearrange("p (h d) -> p h d", h=H),
                                                    rows[:, ROWS["bV"], :].rearrange("p (h d) -> p h d", h=H), ALU.add)
                        ins.then_inc(values_ready["att"], 1)
                    if n == 28 and routed:
                        after(dve, z_out, count(i, 2, 1, 1))
                        after(dve, h1b_ready, count(i, 2, 1, 1))
                        after(dve, out_stored, count(i, 2, DMA, DMA))
                        after(dve, scattered, count(i, 2, T * DMA, DMA))
                        dve.tensor_tensor(h2row[:, :, 0:D], bank[7].rearrange("p (t d) -> p t d", t=T), h1b[:],
                                          ALU.add).then_inc(h2_ready, 1)
                        after(dve, h2_ready, count(i, 2, 1, 1))
                        moments("h2", h2row)
                    if n == 29 and tok:
                        normalise_ctx("tok", i, 0, (5, 6))
                    if n == 30 and routed:
                        deviation("h2").then_inc(h2_stats, 1)
                        dve.tensor_copy(h2row[:, :, D + 2], mv["h2"][:, :, 0])
                        dve.tensor_copy(h2row[:, :, D + 3], rstd["h2"][:])
                    if n == 31 and tok:
                        after(dve, gathered, count(i, 0, T * DMA, 2 * T * DMA))
                        if att:
                            after(dve, turned["att"], count(i, 1, 2 * G, 2 * G))
                        split(xq_parts, xg, x_split)
                    if n == 32 and tok:
                        after(dve, attn_out, count(i, 0, 1, 1))
                        for t in range(T):
                            ins = dve.tensor_tensor(resid[:, t, :].rearrange("p (h d) -> p h d", h=H),
                                                    bank[5][:, t * D:(t + 1) * D].rearrange("p (h d) -> p h d", h=H),
                                                    values["tok"][:, t, :, 0:HD], ALU.add)
                        ins.then_inc(x_added, 1)
                        after(dve, x_added, count(i, 0, 1, 1))
                        moments("x1", resid)
                    if n == 33 and tok:
                        deviation("x1").then_inc(x1_stats, 1)
                    if n == 35 and routed:
                        after(dve, logits, count(i, 2, 1, 1))
                        dve.tensor_copy(lg[:], bank[5][:, 0:T * E].rearrange("p (t e) -> p t e", t=T)
                                        ).then_inc(logits_read, 1)
                        after(dve, logits_read, count(i, 2, 1, 1))
                        link(dve.tensor_reduce(lmax[:], lg[:], AX_X, ALU.max))
                        dve.tensor_tensor(lsh[:], lg[:], spread(lmax), ALU.subtract).then_inc(shifted, 1)
                        link(dve.tensor_tensor(eq[:], lg[:], spread(lmax), ALU.is_equal))
                        link(dve.tensor_tensor(eqr[:], eq[:], rev[:], ALU.mult))
                        link(dve.tensor_reduce(first[:], eqr[:], AX_X, ALU.max))
                        link(dve.tensor_tensor(onehot[:], eqr[:], spread(first), ALU.is_equal))
                        dve.tensor_copy(onehotb[:], onehot[:]).then_inc(onehot_ready, 1)
                    if n == 37 and routed:
                        after(dve, exped, count(i, 2, 1, 1))
                        link(dve.tensor_reduce(lsum[:], lexp[:], AX_X, ALU.add))
                        dve.reciprocal(h2row[:, :, D], lsum[:])
                    if n == 40 and routed:
                        after(dve, ranked, count(i, 2, 1, 1))
                        link(dve.tensor_tensor(posr[:], bank[7][:, 0:T * E].rearrange("p (t e) -> p t e", t=T),
                                               counts[:].rearrange("p (a e) -> p a e", a=1).to_broadcast([P, T, E]),
                                               ALU.add))
                        dve.tensor_tensor(counts[:], counts[:], bank[7][:, T * E:T * E + E],
                                          ALU.add).then_inc(ranks_read, 1)
                        link(dve.tensor_tensor(sel[:], onehot[:], posr[:], ALU.mult))
                        link(dve.tensor_reduce(locf[:], sel[:], AX_X, ALU.add))
                        dve.tensor_scalar(over[:], locf[:], float(CAP), float(NOWHERE), ALU.is_ge, ALU.mult)
                        link(dve.tensor_tensor(sel[:], onehot[:], ebase[:], ALU.mult))
                        link(dve.tensor_reduce(slotf[:], sel[:], AX_X, ALU.add))
                        link(dve.tensor_tensor(slotf[:], slotf[:], locf[:], ALU.add))
                        link(dve.tensor_tensor(slotf[:], slotf[:], over[:], ALU.add))
                        dve.tensor_copy(sloti[:], slotf[:]).then_inc(slot_ready, 1)
                    for pair_of in (1, 3):
                        if n == UP[pair_of][0] + 1 and tok:
                            relu(i, pair_of, UP[pair_of][1])
                return links[2] - at_start

            links[0] = 0
            dve.wait_ge(gathered, T * DMA)
            split(xq_parts, xg, x_split)

            def vectored(i, on):
                if isinstance(i, int):
                    if i == B:
                        links[1], links[2] = 0, links[2] + (B - 2) * STEADY_VECTOR
                    iteration(i, on)
                else:
                    links[1], links[2] = STEADY_VECTOR, links[2] - 2 * STEADY_VECTOR
                    n = iteration(i, on)
                    assert n == STEADY_VECTOR, n
                    links[2] += STEADY_VECTOR

            iterations(dve, vectored)

            with dve.Fori(0, E // 2, 1) as j:
                for k in range(2):
                    e = j * 2 + k
                    dve.wait_ge(e_loaded[k], (j + 1) * (5 * DMA))
                    for t in range(CT):
                        ins = dve.tensor_scalar(xen[:, t, :], xe[:, k, t, 0:D], xe[:, k, t, D + 2:D + 3],
                                                xe[:, k, t, D + 3:D + 4], ALU.subtract, ALU.mult)
                    ins.then_inc(e_normed, 1)
                    dve.wait_ge(e_turned, e + 1)
                    for c in range(C2):
                        ins = dve.tensor_copy(xeT[:, c, :], bank[c])
                    ins.then_inc(eT_ready, 1)
                    for t in range(CT):
                        n = j * (2 * CT) + k * CT + t + 1
                        dve.wait_ge(e_down, n)
                        dve.tensor_tensor(yb[:, t % 2, :], bank[6 + t % 2][:, 0:D], mb2_sb[:, k, :],
                                          ALU.add).then_inc(e_biased, 1)
                        dve.wait_ge(e_biased, n + 1)
                        dve.scalar_tensor_tensor(out=yo[:, k, t, :], in0=yb[:, t % 2, :], scalar=xe[:, k, t, D:D + 1],
                                                 in1=xe[:, k, t, 0:D], op0=ALU.mult, op1=ALU.add).then_inc(e_out, 1)

        @block.tensor
        def _(pe):
            def turn(k, tile, who):
                for c in range(C2):
                    for t in range(T):
                        ins = pe.transpose(bank[k][:, c * S + t * P:c * S + (t + 1) * P],
                                           tile[:, t, c * P:(c + 1) * P], ident[:])
                ins.then_inc(who, 1)

            def project(k, srcT, w, who):
                for t in range(T):
                    for c in range(C2):
                        ins = pe.matmul(bank[k][:, t * D:(t + 1) * D], srcT[:, c, t * P:(t + 1) * P], w[:, c, :],
                                        start=(c == 0), stop=(c == C2 - 1))
                ins.then_inc(who, 1)

            def turn_ctx(s, banks, who):
                for t in range(T):
                    for g in range(G):
                        ins = pe.transpose(bank[banks[t]][:, g * P:(g + 1) * P], CU[:, g, t * P:(t + 1) * P], ident[:])
                    ins.then_inc(who, 1)

            def turn_parts(s, i, m, k, left):
                if left:
                    after(pe, stacked[s], count(i, 0, 2 * G, left))
                parts = xq_parts if s == "tok" or m % 2 else k_parts
                for b in range(2):
                    block_of = 2 * (m // 2) + b
                    for t in range(T):
                        first_place = 1 if parts is xq_parts and m % 2 == 0 else 0
                        src = parts[:, t, block_of, first_place:first_place + 4, :].rearrange("p l w -> p (l w)")
                        ins = pe.transpose(bank[k][:, b * S + t * P:b * S + (t + 1) * P].bitcast(F32R), src, identr[:])
                ins.then_inc(turned[s], 1)

            def core(s, i, n):
                causal = s == "att"
                seq = i - 1 if causal else i
                if 0 <= n < NR:
                    kind, index = RING[n]
                    tile = bank[n % 2]
                    after(pe, ring_read, run_count(s, i, NR, n - 1))
                    if kind == "S":
                        h = index
                        after(pe, stacked[s], count(seq, 0, 2 * G, 2 * (h // 4) + 2))
                        for t in range(T):
                            col, keys = (t * P, (t + 1) * P) if causal else (t * S, S)
                            ins = pe.matmul(tile[:, col:col + keys], QS[s][:, h // 2, t * P:(t + 1) * P],
                                            KS[s][:, h // 2, h % 2, 0:keys], start=True, stop=not causal)
                            if causal:
                                d = col + t * P
                                ins = pe.matmul(tile[:, d:d + P], identb[:], maskq[:], start=False, stop=True)
                    else:
                        after(pe, neg_ready, run_count(s, i, G, index + 1))
                        for t in range(T):
                            ins = pe.transpose(tile[0:4, t * P:(t + 1) * P], negmax[:, t, 4 * index:4 * index + 4],
                                               ident[:])
                    ins.then_inc(ring_filled, 1)
                if n in TURNED_SLOT:
                    h = TURNED_SLOT.index(n)
                    g, r = h // 4, h % 4
                    tile = bank[2 + h % 2]
                    after(pe, ring_read, run_count(s, i, NR, RING.index(("M", g)) + 1))
                    after(pe, probs, run_count(s, i, H, h - 1))
                    pe.matmul(tile.rearrange("p (k q) -> p k q", k=T), identr[:, r:r + 1].to_broadcast([P, P]),
                              negmaxT[:, g:g + 1, :].to_broadcast([P, T, S]), start=True, stop=False,
                              skip_group_check=True)
                    for kt in range(T):
                        q0 = kt * P if causal else 0
                        col = (T - 1 - kt) * S + q0 if causal else kt * S
                        ins = pe.matmul(tile[:, col:col + S - q0], KS[s][:, h // 2, h % 2, kt * P:(kt + 1) * P],
                                        QS[s][:, h // 2, q0:S], start=False, stop=not causal, skip_group_check=True)
                        if causal:
                            ins = pe.matmul(tile[:, col:col + P], identb[:], maskk[:], start=False, stop=True,
                                            skip_group_check=True)
                    ins.then_inc(scores, 1)
                if n in VALUE_SLOT:
                    g = VALUE_SLOT.index(n)
                    after(pe, values_ready[s], count(seq, 0, 1, 1))
                    after(pe, probs, run_count(s, i, H, 4 * g + 4))
                    after(pe, ctx_copied, run_count(s, i, G, g))
                    for kt in range(T):
                        q0 = kt * P if causal else 0
                        col = (T - 1 - kt) * S + q0 if causal else kt * S
                        for r in range(4):
                            ins = pe.matmul(bank[4][32 * r:32 * r + 32, q0:S], values[s][:, kt, 4 * g + r, :],
                                            prob[:, g % 2, r, col:col + S - q0],
                                            start=(kt == 0), stop=(kt == T - 1), skip_group_check=True)
                    ins.then_inc(ctx_done, 1)

            pe.wait_ge(ids_cleaned, 1)
            pe.transpose(bank[7][:, 0:NT], ids_f[:], ident[0:NT, 0:NT]).then_inc(ids_turned, 1)
            pe.wait_ge(ids_ready, 1)
            pe.wait_ge(x_parts, 1)
            for m in range(2 * G):
                turn_parts("tok", 0, m, TOK_BANK[m], TOK_LEFT[m])
            pe.wait_ge(loaded, N_LOADS * DMA)

            def iteration(i, on):
                tok, att, routed = on
                for n in range(SLOTS):
                    if tok:
                        core("tok", i, n)
                    if att:
                        core("att", i, n - ATT_SLOT)
                    if n == 0 and att:
                        after(pe, stacked["tok"], 2 * G * (B + 1) if not tok else count(i, 0, 2 * G, 2 * G))
                    if n in DOWN_SLOT and att:
                        t, half = divmod(DOWN_SLOT.index(n), 2)
                        if t and routed:
                            after(pe, ctx_normed["att"], count(i, 2, T, 1))
                        for f in range(half * NF // 2, (half + 1) * NF // 2):
                            if t == 0:
                                after(pe, relu_dve if f // 2 % 2 else relu_act, count(i, 1, 2, f // 4 + 1))
                            ins = pe.matmul(bank[(7, 5)[t]][:, 0:D], hid[:, f, t * P:(t + 1) * P], w2_sb[:, f, :],
                                            start=(f == 0), stop=(f == NF - 1))
                        if half:
                            ins.then_inc(down_done, 1)
                    if n == 1 and routed:
                        after(pe, ctx_copied, run_count("att", i - 1, G, G))
                        turn_ctx("att", (5, 6), ctx_turned["att"])
                    if n == 13 and att:
                        if routed:
                            after(pe, ctx_normed["att"], count(i, 2, T, T))
                        after(pe, h1_normed, count(i, 1, 1, 1))
                        turn(6, normed_h1, h1_turned)
                    if n == 14 and att:
                        after(pe, h1T_ready, count(i, 1, 1, 1))
                        project(7, h1T, wq_sb, q_proj)
                    if n == 15 and att:
                        project(5, h1T, wk_sb, k_proj)
                    if n == 16 and att:
                        project(6, h1T, wv_sb, v_proj)
                    if n in ATT_TURN_SLOT and att:
                        m = ATT_TURN_SLOT.index(n)
                        if m == 0:
                            after(pe, k_parted, count(i, 1, 1, 1))
                        if m == 1:
                            after(pe, q_parted, count(i, 1, 1, 1))
                        if m == 2:
                            after(pe, values_ready["att"], count(i, 1, 1, 1))
                        turn_parts("att", i - 1, m, ATT_BANK[m], ATT_LEFT[m])
                    if n == 25 and routed:
                        if att:
                            after(pe, stacked["att"], count(i, 1, 2 * G, 6))
                        after(pe, z_ready, count(i, 2, 1, 1))
                        for t in range(T):
                            ins = pe.transpose(bank[6][0:HD, t * P:(t + 1) * P], zsum[:, t, :], ident[:])
                        ins.then_inc(z_turned, 1)
                    if n == 27 and routed:
                        if att:
                            after(pe, stacked["att"], count(i, 1, 2 * G, 7))
                        else:
                            after(pe, ranks_read, count(i, 3, 1, 1))
                        after(pe, zT_ready, count(i, 2, 1, 1))
                        for t in range(T):
                            ins = pe.matmul(bank[7][:, t * D:(t + 1) * D], zT[:, t * P:(t + 1) * P], wo_sb[:],
                                            start=True, stop=True)
                        ins.then_inc(z_out, 1)
                    if n == 28 and tok:
                        after(pe, ctx_copied, run_count("tok", i, G, G))
                        if att:
                            after(pe, stacked["att"], count(i, 1, 2 * G, 2 * G))
                        else:
                            after(pe, stacked["tok"], count(i, 0, 2 * G, 2 * G))
                        turn_ctx("tok", (5, 6), ctx_turned["tok"])
                    if n == 30 and tok:
                        after(pe, ctx_normed["tok"], count(i, 0, T, T))
                        if routed:
                            after(pe, h2_ready, count(i, 2, 1, 1))
                        turn(7, ctxn[:].rearrange("p t h d -> p t (h d)"), ctxnT_turned)
                    if n == 31 and tok:
                        after(pe, ctxnT_ready, count(i, 0, 1, 1))
                        project(5, ctxnT, w_o_sb, attn_out)
                    if n == 32 and routed:
                        after(pe, h2_normed, count(i, 2, 1, 1))
                        turn(6, normed_h2, h2_turned)
                    if n == 34 and routed:
                        after(pe, h2T_ready, count(i, 2, 1, 1))
                        if tok:
                            after(pe, x_added, count(i, 0, 1, 1))
                        for t in range(T):
                            for c in range(C2):
                                ins = pe.matmul(bank[5][:, t * E:(t + 1) * E], h2T[:, c, t * P:(t + 1) * P],
                                                wg_sb[:, c, :], start=(c == 0), stop=(c == C2 - 1))
                        ins.then_inc(logits, 1)
                    if n in TOK_TURN_SLOT and tok:
                        m = TOK_TURN_SLOT.index(n)
                        if m == 0:
                            after(pe, x_parts, count(i, 0, 1, 2))
                        if m == 3 and routed:
                            after(pe, ranks_read, count(i, 2, 1, 1))
                        if m == 5:
                            after(pe, relu_act, count(i, 0, 2, 2))
                        if m == 7:
                            after(pe, relu_dve, count(i, 0, 2, 2))
                        turn_parts("tok", i + 1, m, TOK_BANK[m], TOK_LEFT[m])
                    if n == 36 and tok:
                        if routed:
                            after(pe, logits_read, count(i, 2, 1, 1))
                        after(pe, x1_normed, count(i, 0, 1, 1))
                        turn(5, normed, x1_turned)
                    for pair_of, (slot, k) in enumerate(UP):
                        if n == slot and tok:
                            if pair_of == 0:
                                after(pe, x1T_ready, count(i, 0, 1, 1))
                                after(pe, stacked["tok"], count(i, 0, 2 * G, 2 * G + 2))
                            if pair_of == 2:
                                after(pe, relu_act, count(i, 0, 2, 1))
                            if pair_of == 3:
                                after(pe, relu_dve, count(i, 0, 2, 1))
                            for f in (2 * pair_of, 2 * pair_of + 1):
                                for c in range(C2):
                                    ins = pe.matmul(bank[k][:, (f % 2) * S:(f % 2 + 1) * S],
                                                    w1_sb[:, c, f * P:(f + 1) * P], x1T[:, c, :],
                                                    start=(c == 0), stop=(c == C2 - 1))
                            ins.then_inc(up_done, 1)
                    if n == 39 and routed:
                        after(pe, onehot_ready, count(i, 2, 1, 1))
                        if tok:
                            after(pe, stacked["tok"], count(i, 0, 2 * G, 2 * G + 3))
                        pe.matmul(bank[7][:, 0:E], before[:], onehotb[:, 0, :], start=True, stop=True)
                        pe.matmul(bank[7][:, E:2 * E], before[:], onehotb[:, 1, :], start=True, stop=False)
                        pe.matmul(bank[7][:, E:2 * E], onesb[:], onehotb[:, 0, :], start=False, stop=True)
                        pe.matmul(bank[7][:, 2 * E:3 * E], onesb[:], onehotb[:, 0, :], start=True, stop=False)
                        pe.matmul(bank[7][:, 2 * E:3 * E], onesb[:], onehotb[:, 1, :], start=False, stop=True
                                  ).then_inc(ranked, 1)

            iterations(pe, iteration)

            with pe.Fori(0, E // 2, 1) as j:
                for k in range(2):
                    e = j * 2 + k
                    pe.wait_ge(e_normed, e + 1)
                    for c in range(C2):
                        for t in range(CT):
                            ins = pe.transpose(bank[c][:, t * P:(t + 1) * P], xen[:, t, c * P:(c + 1) * P], ident[:])
                    ins.then_inc(e_turned, 1)
                    pe.wait_ge(eT_ready, e + 1)
                    for f in range(NF):
                        if f >= 4:
                            pe.wait_ge(e_relu, j * (2 * NF) + k * NF + f - 3)
                        for c in range(C2):
                            ins = pe.matmul(bank[2 + f % 4], mw1[k][:, c, f * P:(f + 1) * P], xeT[:, c, :],
                                            start=(c == 0), stop=(c == C2 - 1))
                        ins.then_inc(e_up, 1)
                    pe.wait_ge(e_relu, j * (2 * NF) + k * NF + NF)
                    for t in range(CT):
                        if t >= 2:
                            pe.wait_ge(e_biased, j * (2 * CT) + k * CT + t)
                        else:
                            pe.wait_ge(e_biased, j * (2 * CT) + k * CT + 1)
                        for f in range(NF):
                            ins = pe.matmul(bank[6 + t % 2][:, 0:D], hid[:, f, t * P:(t + 1) * P], mw2[k][:, f, :],
                                            start=(f == 0), stop=(f == NF - 1))
                        ins.then_inc(e_down, 1)


_INS = ["x", "L0_tok_emb", "L0_tok_w_o", "L0_tok_w1", "L0_tok_b1", "L0_tok_w2", "L0_tok_b2", "L0_tok_gamma1",
        "L0_tok_beta1", "L0_tok_gamma2", "L0_tok_beta2", "L0_attn_WQ", "L0_attn_bQ", "L0_attn_WK", "L0_attn_bK",
        "L0_attn_WV", "L0_attn_bV", "L0_attn_WO", "L0_attn_bO", "L0_ffn_Wg", "L0_ffn_W1", "L0_ffn_b1",
        "L0_ffn_W2", "L0_ffn_b2"]
_OUTS = [((16, 256, 256), "float32")]


def kernel(**inputs):
    import numpy as _np
    import concourse.bacc as _bacc
    from concourse import mybir as _mybir
    from concourse.bass_utils import run_bass_kernel_spmd as _run

    nc = _bacc.Bacc("TRN2", target_bir_lowering=False, num_devices=1)
    arrays, args = {}, []
    for name in _INS:
        a = _np.ascontiguousarray(inputs[name])
        arrays[f"in_{name}_dram"] = a
        args.append(nc.dram_tensor(f"in_{name}_dram", a.shape, _mybir.dt.from_np(a.dtype), kind="ExternalInput").ap())
    for i, (shape, dtype) in enumerate(_OUTS):
        dt = _mybir.dt.from_np(_np.dtype(dtype))
        args.append(nc.dram_tensor(f"out_{i}_dram", shape, dt, kind="ExternalOutput").ap())
    lm_tower_kernel(nc, *args)
    r = _run(nc, [arrays], core_ids=[0])
    return r.results[0]["out_0_dram"]
```

```python
from contextlib import ExitStack

import concourse.bass as bass
from concourse import mybir

P = 128
ALU = mybir.AluOpType
ACT = mybir.ActivationFunctionType
F32 = mybir.dt.float32
F32R = mybir.dt.float32r
BF16 = mybir.dt.bfloat16
I32 = mybir.dt.int32
AX_X = mybir.AxisListType.X

EPS = 1e-5
MASKED = -400000.0
ROW_EXTRA = 4
DMA = 16
NEWTON = 3

SLOTS = 54
ATT_SLOT = 26
RING = [("S", 0), ("S", 1), ("S", 2), ("S", 3), ("S", 4), ("S", 5), ("M", 0), ("S", 6), ("S", 7), ("S", 8), ("S", 9),
        ("M", 1), ("S", 10), ("S", 11), ("S", 12), ("S", 13), ("M", 2), ("S", 14), ("S", 15), ("M", 3)]
RING_SLOT = [*range(19), 20]
TURNED_SLOT = [7, 8, 9, 10, 12, 13, 14, 15, 17, 18, 19, 20, 21, 22, 23, 24]
VALUE_SLOT = [12, 17, 22, 27]
ATT_BANK, ATT_LEFT = [7, 5, 6, 7, 5, 6, 7, 5], [0, 0, 0, 1, 2, 3, 4, 5]
TOK_BANK, TOK_LEFT = [7, 6, 7, 7, 7, 7, 7, 6], [0, 0, 1, 3, 4, 5, 6, 2]
ATT_TURN_SLOT = [22, 23, 24, 25, 26, 27, 28, 29]
TOK_TURN_SLOT = [36, 38, 39, 44, 46, 48, 49, 51]
DOWN_SLOT = [0, 2, 4, 5]
UP = [(43, 6), (45, 5), (47, 6), (49, 5)]
STEADY_VECTOR = 41
STEADY_POOL = 55


def lm_tower_kernel(nc, x, emb, w_o, w1, b1, w2, b2, gamma1, beta1, gamma2, beta2,
                    WQ, bQ, WK, bK, WV, bV, WO, bO, Wg, mW1, mb1, mW2, mb2, out):
    B, S = x.shape
    V, D = emb.shape
    F = w1.shape[1]
    E, _, MF = mW1.shape
    HD = WO.shape[0]
    H = D // HD
    T = S // P
    C2 = D // P
    NF = F // P
    N = B * S
    CAP = -(-N // E)
    CT = CAP // P
    G = H // 4
    NB = H // 2
    ROW = D + ROW_EXTRA
    NT = N // P
    NR = len(RING)
    assert (T, C2, NF, HD, CT, G) == (2, 2, 8, 16, 4, 4) and MF == F and B >= 4
    NOWHERE = 1 << 20
    SCALE = float(HD) ** -0.5

    slots_dram = nc.dram_tensor("expert_slots", [E * CAP, ROW], F32).ap()

    with ExitStack() as ctx:
        def sb(name, shape, dt=F32):
            return ctx.enter_context(nc.sbuf_tensor(name, shape, dt))

        def sem(name):
            return ctx.enter_context(nc.semaphore(name))

        bank = [ctx.enter_context(nc.psum_tensor(f"bank{k}", [P, 512], F32))[:] for k in range(8)]

        ident = sb("ident", [P, P])
        identr = sb("identr", [P, P], F32R)
        identb = sb("identb", [P, P], BF16)
        maskq = sb("maskq", [P, P], BF16)
        maskk = sb("maskk", [P, P], BF16)
        before = sb("before", [P, P], BF16)
        onesb = sb("onesb", [P, P], BF16)
        zerob = sb("zerob", [P, P], BF16)
        half_rows = sb("half_rows", [P, 4])
        headmask = sb("headmask", [P, 2])
        w_o_sb = sb("w_o_sb", [P, C2, D])
        w1_sb = sb("w1_sb", [P, C2, F])
        w2_sb = sb("w2_sb", [P, NF, D])
        wq_sb = sb("wq_sb", [P, C2, D])
        wk_sb = sb("wk_sb", [P, C2, D])
        wv_sb = sb("wv_sb", [P, C2, D])
        wg_sb = sb("wg_sb", [P, C2, E])
        wo_sb = sb("wo_sb", [HD, D])
        b1_sb = sb("b1_sb", [P, NF])
        g1c = sb("g1c", [P, C2])
        be1c = sb("be1c", [P, C2])
        ROWS = dict(gamma1=0, beta1=1, b2=2, gamma2=3, beta2=4, bV=5, bO=6, bQ=7, bK=8)
        rows = sb("rows", [P, len(ROWS), D])
        be1b2 = sb("be1b2", [P, D])
        bo16 = sb("bo16", [P, D])
        ids_i = sb("ids_i", [NT, P], I32)
        ids_f = sb("ids_f", [NT, P])
        ids_n = sb("ids_n", [NT, P])
        idx_all = sb("idx_all", [P, NT + T], I32)
        ebase = sb("ebase", [P, T, E])
        rev = sb("rev", [P, T, E])

        gidx = sb("gidx", [P, T], I32)
        xg = sb("xg", [P, T, D])
        values = {s: sb(f"values_{s}", [P, T, H, 32]) for s in ("tok", "att")}
        xq_parts = sb("xq_parts", [P, T, NB, 5, 2 * HD], F32R)
        k_parts = sb("k_parts", [P, T, NB, 4, 2 * HD], F32R)
        unsplit = sb("unsplit", [P, T, D])
        QS = {s: sb(f"QS_{s}", [P, NB, S], F32R) for s in ("tok", "att")}
        KS = {s: sb(f"KS_{s}", [P, NB, 2, S], F32R) for s in ("tok", "att")}
        blockmax = sb("blockmax", [P, 3, H])
        negmax = sb("negmax", [P, T, H])
        negmaxT = sb("negmaxT", [P, G, S + P], F32R)
        prob = sb("prob", [P, 2, 4, 512])
        CU = sb("CU", [P, G, S])
        recip = sb("recip", [P, T, H])
        ctxn = sb("ctxn", [P, T, H, HD])
        feats = sb("feats", [P, 4, C2, S])
        ctxnT, x1T, h1T, h2T = (feats[:, k] for k in range(4))
        hid = sb("hid", [P, NF, CAP])
        resid = sb("resid", [P, T, D])
        normed = sb("normed", [P, T, D])
        normed_h1 = sb("normed_h1", [P, T, D])
        normed_h2 = sb("normed_h2", [P, T, D])
        scaled = sb("scaled", [P, T, D])
        scaled_y = unsplit
        x1b = sb("x1b", [P, T, D])
        h1 = sb("h1", [P, T, D])
        h1b = sb("h1b", [P, T, D])
        empty = h1b[:].rearrange("p t d -> p (t d)")[:, 0:ROW]
        NORMS = ("x1", "y", "h1", "h2")
        stats = sb("stats", [P, T, 6])
        mv = {k: sb(f"mv_{k}", [P, T, 2]) for k in NORMS}
        rstd = {k: sb(f"rstd_{k}", [P, T]) for k in NORMS}
        shift = {k: sb(f"shift_{k}", [P, T]) for k in NORMS}
        var = {k: sb(f"var_{k}", [P, T]) for k in NORMS}
        halved = sb("halved", [P, T], I32)
        corr = sb("corr", [P, T])
        zsum = sb("zsum", [P, T, HD])
        zT = sb("zT", [HD, S])
        h2row = sb("h2row", [P, T, ROW])
        tokid = sb("tokid", [P, T], I32)
        lg = sb("lg", [P, T, E])
        lmax = sb("lmax", [P, T])
        lsh = sb("lsh", [P, T, E])
        lexp = sb("lexp", [P, T, E])
        lsum = sb("lsum", [P, T])
        eq = sb("eq", [P, T, E])
        eqr = sb("eqr", [P, T, E])
        first = sb("first", [P, T])
        onehot = sb("onehot", [P, T, E])
        onehotb = sb("onehotb", [P, T, E], BF16)
        posr = sb("posr", [P, T, E])
        sel = sb("sel", [P, T, E])
        locf = sb("locf", [P, T])
        slotf = sb("slotf", [P, T])
        over = sb("over", [P, T])
        sloti = sb("sloti", [P, T], I32)
        counts = sb("counts", [P, E])
        xe = sb("xe", [P, 2, CT, ROW])
        xen = CU[:]
        xeT = values["tok"][:].rearrange("p t h w -> p (t h w)").rearrange("p (c n) -> p c n", c=C2)
        mw1 = [w1_sb, feats[:].rearrange("p k c s -> p (k c s)").rearrange("p (c f) -> p c f", c=C2)]
        mw2 = [w2_sb, sb("mw2", [P, NF, D])]
        mb1_sb = sb("mb1_sb", [P, 2, NF])
        mb2_sb, yb = scaled, unsplit
        yo = prob[:, :, :, 0:D]

        loaded = sem("loaded")
        ids_loaded = sem("ids_loaded")
        pool_const = sem("pool_const")
        vec_const = sem("vec_const")
        ids_cleaned = sem("ids_cleaned")
        ids_turned = sem("ids_turned")
        ids_ready = sem("ids_ready")
        vector_step = sem("vector_step")
        pool_step = sem("pool_step")
        ring_filled = sem("ring_filled")
        maxed = sem("maxed")
        neg_ready = sem("neg_ready")
        negT_ready = sem("negT_ready")
        scores = sem("scores")
        probs = sem("probs")
        ctx_done = sem("ctx_done")
        ctx_copied = sem("ctx_copied")
        moments_ready = {k: sem(f"moments_ready_{k}") for k in NORMS}
        rstd_ready = {k: sem(f"rstd_ready_{k}") for k in NORMS}
        ctx_turned = {s: sem(f"ctx_turned_{s}") for s in ("tok", "att")}
        ctx_normed = {s: sem(f"ctx_normed_{s}") for s in ("tok", "att")}
        turned = {s: sem(f"turned_{s}") for s in ("tok", "att")}
        stacked = {s: (sem(f"stacked_k_{s}"), sem(f"stacked_q_{s}")) for s in ("tok", "att")}
        values_ready = {s: sem(f"values_ready_{s}") for s in ("tok", "att")}
        gathered = sem("gathered")
        x_split, x_parts = sem("x_split"), sem("x_parts")
        ctxnT_turned = sem("ctxnT_turned")
        ctxnT_ready = sem("ctxnT_ready")
        attn_out = sem("attn_out")
        x_added = sem("x_added")
        x1_normed = sem("x1_normed")
        x1_turned = sem("x1_turned")
        x1T_ready = sem("x1T_ready")
        x1b_ready = sem("x1b_ready")
        up_done = sem("up_done")
        relu_act = sem("relu_act")
        relu_dve = sem("relu_dve")
        down_done = sem("down_done")
        y_added = sem("y_added")
        h1_ready = sem("h1_ready")
        h1_normed = sem("h1_normed")
        h1_turned = sem("h1_turned")
        h1T_ready = sem("h1T_ready")
        h1b_ready = sem("h1b_ready")
        q_proj, k_proj, v_proj = sem("q_proj"), sem("k_proj"), sem("v_proj")
        q_ready, k_ready = sem("q_ready"), sem("k_ready")
        q_split, k_split = sem("q_split"), sem("k_split")
        q_parted, k_parted = sem("q_parted"), sem("k_parted")
        z_ready = sem("z_ready")
        z_turned = sem("z_turned")
        zT_ready = sem("zT_ready")
        z_out = sem("z_out")
        h2_ready = sem("h2_ready")
        h2_normed = sem("h2_normed")
        h2_turned = sem("h2_turned")
        h2T_ready = sem("h2T_ready")
        logits = sem("logits")
        logits_read = sem("logits_read")
        shifted = sem("shifted")
        exped = sem("exped")
        onehot_ready = sem("onehot_ready")
        ranked = sem("ranked")
        ranks_read = sem("ranks_read")
        slot_ready = sem("slot_ready")
        tokid_ready = sem("tokid_ready")
        out_stored = sem("out_stored")
        scattered = sem("scattered")
        e_loaded = [sem("e_loaded0"), sem("e_loaded1")]
        e_normed = sem("e_normed")
        e_turned = sem("e_turned")
        eT_ready = sem("eT_ready")
        e_up = sem("e_up")
        e_relu = sem("e_relu")
        e_down = sem("e_down")
        e_biased = sem("e_biased")
        e_out = sem("e_out")
        e_scattered = [sem("e_scattered0"), sem("e_scattered1")]

        out_rows = out.rearrange("b (t p) d -> p b t d", p=P).rearrange("p b t d -> p (b t) d")
        flat_out = out.rearrange("b s d -> (b s) d")

        passed = sem("passed")

        def after(eng, semaphore, value):
            if not isinstance(value, int) or value > 0:
                eng.wait_ge(semaphore, value)

        def after_apart(eng, semaphore, value):
            if not isinstance(value, int) or value > 0:
                eng.wait_ge(semaphore, value)
                eng.sem_inc(passed, 1)

        def count(i, lag, per, c):
            return i * per + (c - lag * per)

        def turn_left(eng, s, i, lag, n):
            after(eng, stacked[s][n % 2], count(i, lag, G, n // 2 + 1))

        def turns_left(eng, s, i, lag):
            for n in (2 * G - 2, 2 * G - 1):
                turn_left(eng, s, i, lag, n)

        def run_count(s, i, per, c):
            if isinstance(i, int) and i in (0, B):
                return (2 * i - (i == B)) * per + c
            return i * (2 * per) + ((-1 if s == "tok" else 0) * per + c)

        def first_run(i, per, c):
            return run_count("att" if isinstance(i, int) and i == B else "tok", i, per, c)

        def active(i, steady):
            return (True, True, True) if steady else (i < B, 1 <= i <= B, 2 <= i)

        def iterations(eng, body):
            for i in (0, 1):
                body(i, active(i, False))
            with eng.Fori(2, B, 1) as i:
                body(i, active(i, True))
            for i in (B, B + 1):
                body(i, active(i, False))

        def experts(eng, body):
            with eng.Fori(0, E // 2 - 1, 1) as j:
                for k in range(2):
                    body(j, k, True)
            for k in range(2):
                body(E // 2 - 1, k, k == 0)

        block = ctx.enter_context(nc.Block())

        N_LOADS = 20

        @block.sync
        def _(sp):
            sp.dma_start(ids_i[:], x.rearrange("b (t p) -> (b t) p", p=P)).then_inc(ids_loaded, DMA)

            def load(dst, src):
                sp.dma_start(dst, src).then_inc(loaded, DMA)

            with nc.allow_non_contiguous_dma(reason="a few bias columns"):
                load(b1_sb[:], b1.rearrange("(f p) -> p f", p=P))
                load(g1c[:], gamma1.rearrange("(c p) -> p c", p=P))
                load(be1c[:], beta1.rearrange("(c p) -> p c", p=P))
            for k, r in enumerate((gamma1, beta1, b2, gamma2, beta2, bV, bO, bQ, bK)):
                load(rows[:, k, :], r.rearrange("(a d) -> a d", a=1).to_broadcast([P, D]))
            load(w_o_sb[:], w_o.rearrange("(c p) n -> p c n", p=P))
            load(w1_sb[:], w1.rearrange("(c p) n -> p c n", p=P))
            load(w2_sb[:], w2.rearrange("(c p) n -> p c n", p=P))
            load(wq_sb[:], WQ.rearrange("(c p) n -> p c n", p=P))
            load(wk_sb[:], WK.rearrange("(c p) n -> p c n", p=P))
            load(wv_sb[:], WV.rearrange("(c p) n -> p c n", p=P))
            load(wo_sb[:], WO)
            load(wg_sb[:], Wg.rearrange("(c p) n -> p c n", p=P))

            sp.sem_inc(out_stored, DMA)

            def iteration(i, on):
                if on[2]:
                    after(sp, h2_ready, count(i, 2, 1, 1))
                    sp.dma_start(out_rows[:, bass.ds(count(i, 2, T, 0), T), :], h2row[:, :, 0:D]).then_inc(out_stored, DMA)

            def load_rows(e, k):
                sp.dma_start(xe[:, k], slots_dram.rearrange("(e t p) r -> e p t r", t=CT, p=P)[e]
                             ).then_inc(e_loaded[k], DMA)

            def load_weights(e, k):
                w = e_loaded[k]
                sp.dma_start(mw1[k][:], mW1.rearrange("e (c p) f -> e p c f", p=P)[e]).then_inc(w, DMA)
                sp.dma_start(mw2[k][:], mW2.rearrange("e (c p) f -> e p c f", p=P)[e]).then_inc(w, DMA)
                with nc.allow_non_contiguous_dma(reason="bias columns"):
                    sp.dma_start(mb1_sb[:, k], mb1.rearrange("e (f p) -> e p f", p=P)[e]).then_inc(w, DMA)
                sp.dma_start(mb2_sb[:, k], mb2.rearrange("e (a d) -> e a d", a=1)[e].to_broadcast([P, D])).then_inc(w, DMA)

            def routed_rows(i, on):
                iteration(i, on)
                if isinstance(i, int) and i == B:
                    sp.wait_ge(y_added, T * B)
                    load_weights(0, 0)

            iterations(sp, routed_rows)
            sp.wait_ge(scattered, DMA * T * B + DMA)
            load_rows(0, 0)
            load_rows(1, 1)
            load_weights(1, 1)
            with sp.Fori(0, E // 2 - 1, 1) as j:
                for k in range(2):
                    sp.wait_ge(e_scattered[k], (j + 1) * (CT * DMA))
                    load_rows(2 * j + 2 + k, k)
                    load_weights(2 * j + 2 + k, k)

        @block.gpsimd
        def _(pool):
            pool.memset(empty[:], 0.0).then_inc(pool_const, 1)
            pool.wait_ge(pool_const, 1)
            pool.memset(empty[:].bitcast(I32)[:, D + 1:D + 2], NOWHERE).then_inc(pool_const, 1)
            pool.memset(ident[:], 0.0).then_inc(pool_const, 1)
            pool.memset(idx_all[:], 0).then_inc(pool_const, 1)
            pool.memset(onesb[:], 1.0).then_inc(pool_const, 1)
            pool.memset(zerob[:], 0.0).then_inc(pool_const, 1)
            pool.memset(half_rows[:], 1.0).then_inc(pool_const, 1)
            pool.memset(CU[:], 0.0).then_inc(pool_const, 1)
            pool.memset(values["tok"][:], 0.0).then_inc(pool_const, 1)
            pool.memset(values["att"][:], 0.0).then_inc(pool_const, 1)
            pool.memset(counts[:], 0.0).then_inc(pool_const, 1)
            pool.wait_ge(pool_const, 11)
            for s in ("tok", "att"):
                pool.memset(values[s][:, :, :, HD:HD + 1], 1.0).then_inc(pool_const, 1)
            pool.affine_select(out=ident[:], in_=ident[:], compare_op=ALU.not_equal, fill=1.0, base=0,
                               pattern=[[-1, P]], channel_multiplier=1).then_inc(pool_const, 1)
            pool.affine_select(out=maskq[:], in_=zerob[:], compare_op=ALU.is_ge, fill=MASKED, base=0,
                               pattern=[[-1, P]], channel_multiplier=1).then_inc(pool_const, 1)
            pool.affine_select(out=maskk[:], in_=zerob[:], compare_op=ALU.is_ge, fill=MASKED, base=0,
                               pattern=[[1, P]], channel_multiplier=-1).then_inc(pool_const, 1)
            pool.affine_select(out=before[:], in_=onesb[:], compare_op=ALU.is_gt, fill=0.0, base=0,
                               pattern=[[1, P]], channel_multiplier=-1).then_inc(pool_const, 1)
            pool.affine_select(out=half_rows[:], in_=half_rows[:], compare_op=ALU.is_ge, fill=0.0, base=0,
                               pattern=[[-32, 4]], channel_multiplier=1).then_inc(pool_const, 1)
            pool.wait_ge(pool_const, 18)
            pool.affine_select(out=half_rows[:], in_=half_rows[:], compare_op=ALU.is_ge, fill=0.0, base=HD - 1,
                               pattern=[[32, 4]], channel_multiplier=-1).then_inc(pool_const, 1)
            pool.iota(tokid[:], pattern=[[P, T]], base=-S, channel_multiplier=1).then_inc(pool_const, 1)
            pool.iota(ebase[:], pattern=[[0, T], [CAP, E]], base=0, channel_multiplier=0,
                      allow_small_or_imprecise_dtypes=True).then_inc(pool_const, 1)
            pool.iota(rev[:], pattern=[[0, T], [-1, E]], base=E, channel_multiplier=0,
                      allow_small_or_imprecise_dtypes=True).then_inc(pool_const, 1)
            pool.tensor_copy(identb[:], ident[:]).then_inc(pool_const, 1)

            steps = [0, 0]

            def link(ins, i):
                ins.then_inc(pool_step, 1)
                steps[1] += 1
                after_apart(pool, pool_step, i * steps[0] + steps[1])

            def gather(i, now):
                link(pool.tensor_copy(gidx[:], idx_all[:, bass.ds(i * T, T)]), now)
                for t in range(T):
                    pool.indirect_dma_start(xg[:, t, :], None, emb, bass.IndirectOffsetOnAxis(gidx[:, t:t + 1], 0)
                                            ).then_inc(gathered, DMA)

            def take_values(i):
                after_apart(pool, gathered, count(i, 0, T * DMA, T * DMA))
                pool.tensor_copy(values["tok"][:, :, :, 0:HD],
                                 xg[:].rearrange("p t (h d) -> p t h d", h=H)).then_inc(values_ready["tok"], 1)

            def deviation(k, i, n):
                after_apart(pool, moments_ready[k], n)
                for _ in range(NEWTON):
                    link(pool.tensor_tensor(corr[:], rstd[k][:], rstd[k][:], ALU.mult), i)
                    link(pool.tensor_tensor(corr[:], corr[:], var[k][:], ALU.mult), i)
                    link(pool.tensor_scalar(corr[:], corr[:], -0.5, 1.5, ALU.mult, ALU.add), i)
                    link(pool.tensor_tensor(rstd[k][:], corr[:], rstd[k][:], ALU.mult), i)
                link(pool.tensor_tensor(shift[k][:], mv[k][:, :, 0], rstd[k][:], ALU.mult), i)
                pool.tensor_scalar(shift[k][:], shift[k][:], -1.0, None, ALU.mult).then_inc(rstd_ready[k], 1)

            pool.wait_ge(ids_ready, 1)
            gather(0, 0)
            take_values(0)
            pool.dma_start(slots_dram.rearrange("(p s) r -> p s r", p=P),
                           empty[:].rearrange("p (a r) -> p a r", a=1).to_broadcast([P, E * CAP // P, ROW])
                           ).then_inc(scattered, DMA)
            pool.wait_ge(loaded, N_LOADS * DMA)
            pool.wait_ge(vec_const, 10)
            pool.wait_ge(scattered, DMA)

            def iteration(i, on):
                tok, att, routed = on
                at_start = steps[1]
                if tok:
                    after_apart(pool, values_ready["tok"], count(i, 0, 1, 1))
                    after_apart(pool, x_split, count(i, 0, 1, 1))
                    gather(i + 1, i)
                if att:
                    deviation("y", i, count(i, 1, 1, 1))
                if att:
                    deviation("h1", i, count(i, 1, 1, 1))
                    if routed:
                        after_apart(pool, h2_ready, count(i, 2, 1, 1))
                    after_apart(pool, h1_ready, count(i, 1, 1, 1))
                    for t in range(T):
                        ins = pool.tensor_tensor(h1b[:, t, :], h1[:, t, :], bo16[:], ALU.add)
                    ins.then_inc(h1b_ready, 1)
                if routed:
                    deviation("h2", i, count(i, 2, 1, 1))
                if tok:
                    deviation("x1", i, count(i, 0, 1, 1))
                    after_apart(pool, x1_normed, count(i, 0, 1, 1))
                    for t in range(T):
                        ins = pool.tensor_tensor(scaled[:, t, :], normed[:, t, :], rows[:, ROWS["gamma1"], :], ALU.mult)
                    link(ins, i)
                    for t in range(T):
                        ins = pool.tensor_tensor(x1b[:, t, :], scaled[:, t, :], be1b2[:], ALU.add)
                    ins.then_inc(x1b_ready, 1)
                    after_apart(pool, x_added, count(i, 0, 1, 1))
                    take_values(i + 1)
                if routed:
                    link(pool.tensor_scalar(tokid[:], tokid[:], float(S), None, ALU.add), i)
                    after_apart(pool, scattered, count(i, 2, T * DMA, DMA))
                    pool.tensor_copy(h2row[:, :, D + 1:D + 2].bitcast(I32),
                                     tokid[:].rearrange("p (t a) -> p t a", a=1)).then_inc(tokid_ready, 1)
                    after_apart(pool, slot_ready, count(i, 2, 1, 1))
                    after_apart(pool, tokid_ready, count(i, 2, 1, 1))
                    for t in range(T):
                        pool.indirect_dma_start(slots_dram, bass.IndirectOffsetOnAxis(sloti[:, t:t + 1], 0),
                                                h2row[:, t, :], None, bounds_check=E * CAP - 1,
                                                oob_is_err=False).then_inc(scattered, DMA)
                return steps[1] - at_start

            def pooled(i, on):
                if isinstance(i, int):
                    if i == B and steps[0]:
                        steps[0], steps[1] = 0, steps[1] + (B - 2) * STEADY_POOL
                    iteration(i, on)
                else:
                    steps[0], steps[1] = STEADY_POOL, steps[1] - 2 * STEADY_POOL
                    assert iteration(i, on) == STEADY_POOL
                    steps[1] += STEADY_POOL

            iterations(pool, pooled)

            pool.wait_ge(out_stored, B * DMA + DMA)
            with pool.Fori(0, E // 2, 1) as j:
                for k in range(2):
                    for t in range(CT):
                        after_apart(pool, e_out, j * (2 * CT) + k * CT + t + 1)
                        pool.indirect_dma_start(flat_out, bass.IndirectOffsetOnAxis(
                            xe[:, k, t, D + 1:D + 2].bitcast(I32), 0), yo[:, k, t, :], None,
                            bounds_check=N - 1, oob_is_err=False).then_inc(e_scattered[k], DMA)
            pool.wait_ge(gathered, (B + 1) * T * DMA)
            for k in range(2):
                pool.wait_ge(e_scattered[k], E // 2 * CT * DMA)

        @block.scalar
        def _(act):
            def core(s, i, n):
                if n in RING_SLOT and RING[RING_SLOT.index(n)][0] == "M":
                    place = RING_SLOT.index(n)
                    width = S if s == "tok" else S + P
                    after(act, ring_filled, run_count(s, i, NR, place + 1))
                    act.activation(negmaxT[0:4, RING[place][1], 0:width], bank[place % 2][0:4, 0:width],
                                   ACT.Copy).then_inc(negT_ready, 1)
                if n in TURNED_SLOT:
                    h = TURNED_SLOT.index(n)
                    g, r = h // 4, h % 4
                    after(act, scores, run_count(s, i, H, h + 1))
                    after(act, ctx_done, run_count(s, i, G, g - 1))
                    a = 0 if s == "tok" else P
                    act.activation(prob[:, g % 2, r, a:], bank[2 + h % 2][:, a:], ACT.Exp,
                                   scale=SCALE).then_inc(probs, 1)
                if n in VALUE_SLOT:
                    g = VALUE_SLOT.index(n)
                    after(act, ctx_done, run_count(s, i, G, g + 1))
                    if g == 0:
                        if s == "tok":
                            after(act, ctx_turned["att"], count(i, 2, T, T))
                        elif i < B if isinstance(i, int) else True:
                            after(act, ctx_turned["tok"], count(i, 0, T, T))
                    act.activation(CU[:, g, :], bank[4][:, 0:S], ACT.Copy).then_inc(ctx_copied, 1)

            def stack(s, i, m, k):
                after(act, turned[s], count(i, 0, 2 * G, m + 1))
                b = 2 * (m // 2)
                src = bank[k].rearrange("p (b q) -> p b q", b=2)
                for r in range(2):
                    ins = act.activation(KS[s][:, b:b + 2, r, :], src, ACT.Copy, scale=headmask[:, r:r + 1])
                ins.then_inc(stacked[s][0], 1)

            def apply(k, dst, src):
                for t in range(T):
                    ins = act.activation(dst[:, t, :], src[:, t, :], ACT.Identity,
                                         bias=shift[k][:, t:t + 1], scale=rstd[k][:, t:t + 1])
                return ins

            def leave(dst, k):
                return act.activation(dst, bank[k].rearrange("p (c q) -> p c q", c=C2), ACT.Copy)

            def relu(i, pair_of, k):
                after(act, up_done, count(i, 0, NF // 2, pair_of + 1))
                for f in (2 * pair_of, 2 * pair_of + 1):
                    ins = act.activation(hid[:, f, 0:S], bank[k][:, (f % 2) * S:(f % 2 + 1) * S],
                                         ACT.Relu, bias=b1_sb[:, f:f + 1])
                ins.then_inc(relu_act, 1)

            def repeat(parts, places, who):
                flat = parts[:].rearrange("p t b l w -> p (t b) l w")
                for src, dst in places:
                    ins = act.activation(flat[:, :, dst, :], flat[:, :, src, :], ACT.Copy)
                ins.then_inc(who, 1)

            act.wait_ge(vec_const, 10)
            act.wait_ge(x_split, 1)
            repeat(xq_parts, ((1, 4), (2, 3), (1, 0)), x_parts)
            for m in range(0, 2 * G, 2):
                stack("tok", 0, m, TOK_BANK[m])
            act.wait_ge(loaded, N_LOADS * DMA)

            def iteration(i, on):
                tok, att, routed = on
                for n in range(SLOTS):
                    if tok:
                        core("tok", i, n)
                    if att:
                        core("att", i, n - ATT_SLOT)
                    if n == 16 and att:
                        after(act, rstd_ready["h1"], count(i, 1, 1, 1))
                        apply("h1", normed_h1, h1).then_inc(h1_normed, 1)
                    if n == 17 and att:
                        after(act, h1_turned, count(i, 1, 1, 1))
                        leave(h1T, 6).then_inc(h1T_ready, 1)
                    if n == 19 and att:
                        after(act, q_split, count(i, 1, 1, 1))
                        repeat(xq_parts, ((1, 0), (2, 3)), q_parted)
                    if n == 20 and att:
                        after(act, k_split, count(i, 1, 1, 1))
                        repeat(k_parts, ((1, 2), (0, 3)), k_parted)
                    if n in ATT_TURN_SLOT and att:
                        m = ATT_TURN_SLOT.index(n)
                        if m % 2 == 0:
                            stack("att", i - 1, m, ATT_BANK[m])
                    if n == 6 and routed:
                        after(act, z_turned, count(i, 2, 1, 1))
                        act.activation(zT[:], bank[6][0:HD, 0:S], ACT.Copy).then_inc(zT_ready, 1)
                    if n == 34 and tok:
                        after(act, ctxnT_turned, count(i, 0, 1, 1))
                        leave(ctxnT, 7).then_inc(ctxnT_ready, 1)
                    if n == 30 and routed:
                        after(act, rstd_ready["h2"], count(i, 2, 1, 1))
                        apply("h2", normed_h2, h2row[:, :, 0:D]).then_inc(h2_normed, 1)
                    if n == 35 and tok:
                        after(act, x_split, count(i, 0, 1, 2))
                        repeat(xq_parts, ((1, 4), (2, 3), (1, 0)), x_parts)
                    if n == 33 and routed:
                        after(act, h2_turned, count(i, 2, 1, 1))
                        leave(h2T, 6).then_inc(h2T_ready, 1)
                    if n == 40 and tok:
                        after(act, rstd_ready["x1"], count(i, 0, 1, 1))
                        after(act, x1b_ready, i)
                        apply("x1", normed, resid).then_inc(x1_normed, 1)
                    if n == 39 and routed:
                        after(act, shifted, count(i, 2, 1, 1))
                        act.activation(lexp[:], lsh[:], ACT.Exp).then_inc(exped, 1)
                    if n == 42 and tok:
                        after(act, x1_turned, count(i, 0, 1, 1))
                        for c in range(C2):
                            ins = act.activation(x1T[:, c, :], bank[5][:, c * S:(c + 1) * S], ACT.Identity,
                                                 bias=be1c[:, c:c + 1], scale=g1c[:, c:c + 1])
                        ins.then_inc(x1T_ready, 1)
                    for pair_of in (0, 2):
                        if n == UP[pair_of][0] + 1 and tok:
                            relu(i, pair_of, UP[pair_of][1])
                    if n in TOK_TURN_SLOT and tok:
                        m = TOK_TURN_SLOT.index(n)
                        if m % 2 == 0:
                            stack("tok", i + 1, m, TOK_BANK[m])

            iterations(act, iteration)

            with act.Fori(0, E // 2, 1) as j:
                for k in range(2):
                    for f in range(NF):
                        act.wait_ge(e_up, j * (2 * NF) + k * NF + f + 1)
                        act.activation(hid[:, f, :], bank[2 + f % 4], ACT.Relu,
                                       bias=mb1_sb[:, k, f:f + 1]).then_inc(e_relu, 1)

        @block.vector
        def _(dve):
            done = [0]

            def const(ins):
                ins.then_inc(vec_const, 1)
                done[0] += 1
                dve.wait_ge(vec_const, done[0])

            dve.sem_inc(e_biased, 1)
            dve.wait_ge(pool_const, 23)
            const(dve.tensor_reduce(headmask[:, 0:1], half_rows[:], AX_X, ALU.add))
            const(dve.tensor_scalar(headmask[:, 1:2], headmask[:, 0:1], -1.0, 1.0, ALU.mult, ALU.add))
            const(dve.tensor_copy(identr[:], ident[:]))
            for g in range(G):
                ins = dve.tensor_copy(negmaxT[:, g, :], CU[:].rearrange("p g s -> p (g s)")[:, 0:S + P])
            const(ins)
            dve.wait_ge(ids_loaded, DMA)
            const(dve.tensor_copy(ids_f[:], ids_i[:]))
            const(dve.tensor_scalar(ids_n[:], ids_f[:], 0.0, float(V), ALU.is_lt, ALU.mult))
            const(dve.tensor_tensor(ids_f[:], ids_f[:], ids_n[:], ALU.add))
            const(dve.tensor_scalar(ids_f[:], ids_f[:], float(V - 1), 0.0, ALU.min, ALU.max))
            dve.sem_inc(ids_cleaned, 1)
            dve.wait_ge(ids_turned, 1)
            dve.tensor_copy(idx_all[:, 0:NT], bank[7][:, 0:NT]).then_inc(ids_ready, 1)
            dve.wait_ge(loaded, N_LOADS * DMA)
            const(dve.tensor_tensor(be1b2[:], rows[:, ROWS["beta1"], :], rows[:, ROWS["b2"], :], ALU.add))
            const(dve.tensor_scalar(bo16[:], rows[:, ROWS["bO"], :], float(H), None, ALU.mult))

            links = [None, 0, 0]

            def link(ins, apart=False):
                ins.then_inc(vector_step, 1)
                links[2] += 1
                (after_apart if apart else after)(dve, vector_step, links[0] * links[1] + links[2])

            def moments(k, src):
                for t in range(T):
                    ins = dve.bn_stats(stats[:, t, :], src[:, t, 0:D])
                link(ins, apart=True)
                for t in range(T):
                    ins = dve.bn_aggr(mv[k][:, t, :], stats[:, t, :])
                link(ins)
                link(dve.tensor_scalar(var[k][:], mv[k][:, :, 1], EPS, None, ALU.add))
                link(dve.tensor_scalar(halved[:], var[k][:].bitcast(I32), 1, None, ALU.logical_shift_right))
                dve.tensor_scalar(rstd[k][:].bitcast(I32), halved[:], -1.0, float(0x5F3759DF), ALU.mult,
                                  ALU.add).then_inc(moments_ready[k], 1)

            def core(s, i, n):
                if n not in RING_SLOT:
                    return
                n = RING_SLOT.index(n)
                kind, index = RING[n]
                if kind == "M":
                    return
                after(dve, ring_filled, run_count(s, i, NR, n + 1))
                h = index
                if s == "tok":
                    src, dst = bank[n % 2].rearrange("p (t k) -> p t k", t=T), blockmax[:, 0:T, h]
                else:
                    src, dst = bank[n % 2][:, 0:3 * P].rearrange("p (b k) -> p b k", b=3), blockmax[:, :, h]
                dve.tensor_reduce(dst, src, AX_X, ALU.max).then_inc(maxed, 1)
                if h % 4 == 3:
                    after(dve, maxed, run_count(s, i, H, h + 1))
                    heads = slice(h - 3, h + 1)
                    if s == "att":
                        link(dve.tensor_tensor(blockmax[:, 1, heads], blockmax[:, 1, heads],
                                               blockmax[:, 2, heads], ALU.max))
                    dve.tensor_scalar(negmax[:, :, heads], blockmax[:, 0:T, heads], -1.0, None,
                                      ALU.mult).then_inc(neg_ready, 1)

            def normalise_ctx(s, i, lag, banks):
                for t in range(T):
                    after(dve, ctx_turned[s], count(i, lag, T, t + 1))
                    tile = bank[banks[t]].rearrange("p (h w) -> p h w", w=32)
                    link(dve.reciprocal(recip[:, t, :], tile[:, :, HD]))
                    dve.tensor_tensor(ctxn[:, t], tile[:, :, 0:HD],
                                      recip[:, t, :].rearrange("p (h a) -> p h a", a=1).to_broadcast([P, H, HD]),
                                      ALU.mult).then_inc(ctx_normed[s], 1)

            def split(dst, src, who):
                a = 1 if dst is xq_parts else 0
                flat, src = dst[:].rearrange("p t b l w -> p (t b) l w"), src[:].rearrange("p t (b w) -> p (t b) w", b=NB)
                link(dve.tensor_copy(flat[:, :, a, :], src))
                dve.tensor_tensor(flat[:, :, a + 1, :], src, flat[:, :, a, :].bitcast(F32),
                                  ALU.subtract).then_inc(who, 1)

            def biased(k, bias):
                return (bank[k].rearrange("p (t d) -> p t d", t=T),
                        rows[:, ROWS[bias]:ROWS[bias] + 1, :].to_broadcast([P, T, D]))

            def stack(s, i, m, k):
                after(dve, turned[s], count(i, 0, 2 * G, m + 1))
                dve.tensor_copy(QS[s][:, m - 1:m + 1, :], bank[k].rearrange("p (b q) -> p b q", b=2)
                                ).then_inc(stacked[s][1], 1)

            def relu(i, pair_of, k):
                after(dve, up_done, count(i, 0, NF // 2, pair_of + 1))
                for f in (2 * pair_of, 2 * pair_of + 1):
                    ins = dve.tensor_scalar(hid[:, f, 0:S], bank[k][:, (f % 2) * S:(f % 2 + 1) * S],
                                            b1_sb[:, f:f + 1], 0.0, ALU.add, ALU.max)
                ins.then_inc(relu_dve, 1)

            def spread(stat):
                return stat[:].rearrange("p (t a) -> p t a", a=1).to_broadcast([P, T, E])

            def iteration(i, on):
                tok, att, routed = on
                links[0] = i
                at_start = links[2]
                for n in range(SLOTS):
                    if tok:
                        core("tok", i, n)
                    if att:
                        core("att", i, n - ATT_SLOT)
                    if n == 2 and routed:
                        normalise_ctx("att", i, 2, (5, 6))
                        after(dve, ctx_normed["att"], count(i, 2, T, T))
                        dve.tensor_reduce(zsum[:], ctxn[:].rearrange("p t h d -> p t d h"), AX_X,
                                          ALU.add).then_inc(z_ready, 1)
                    if n in (3, 6) and att:
                        t = n // 6
                        after(dve, down_done, count(i, 1, T, t + 1))
                        if t == 0:
                            after(dve, x1b_ready, count(i, 1, 1, 1))
                        dve.tensor_tensor(resid[:, t, :], bank[(7, 5)[t]][:, 0:D], x1b[:, t, :], ALU.add
                                          ).then_inc(y_added, 1)
                        if t == T - 1:
                            after(dve, y_added, count(i, 1, T, T))
                            moments("y", resid)
                    if n == 11 and att:
                        if routed:
                            after(dve, h1b_ready, count(i, 2, 1, 1))
                            after(dve, h1_normed, count(i, 2, 1, 1))
                        after(dve, rstd_ready["y"], count(i, 1, 1, 1))
                        for t in range(T):
                            ins = dve.scalar_tensor_tensor(out=scaled_y[:, t, :], in0=resid[:, t, :],
                                                           scalar=mv["y"][:, t, 0:1], in1=rows[:, ROWS["gamma2"], :],
                                                           op0=ALU.subtract, op1=ALU.mult)
                        link(ins)
                        for t in range(T):
                            ins = dve.scalar_tensor_tensor(out=h1[:, t, :], in0=scaled_y[:, t, :],
                                                           scalar=rstd["y"][:, t:t + 1], in1=rows[:, ROWS["beta2"], :],
                                                           op0=ALU.mult, op1=ALU.add)
                        ins.then_inc(h1_ready, 1)
                    if n == 12 and att:
                        after(dve, h1_ready, count(i, 1, 1, 1))
                        moments("h1", h1)
                    if n == 18 and att:
                        after(dve, q_proj, count(i, 1, 1, 1))
                        after(dve, turned["tok"], count(i, 0, 2 * G, 2 * G))
                        dve.tensor_tensor(unsplit[:], *biased(7, "bQ"), ALU.add).then_inc(q_ready, 1)
                        after(dve, q_ready, count(i, 1, 1, 1))
                        split(xq_parts, unsplit, q_split)
                    if n == 19 and att:
                        after(dve, k_proj, count(i, 1, 1, 1))
                        after(dve, q_split, count(i, 1, 1, 1))
                        after(dve, turned["att"], count(i, 1, 2 * G, 0))
                        dve.tensor_tensor(unsplit[:], *biased(5, "bK"), ALU.add).then_inc(k_ready, 1)
                        after(dve, k_ready, count(i, 1, 1, 1))
                        split(k_parts, unsplit, k_split)
                    if n == 20 and att:
                        after(dve, v_proj, count(i, 1, 1, 1))
                        after(dve, ctx_done, first_run(i, G, 0))
                        for t in range(T):
                            ins = dve.tensor_tensor(values["att"][:, t, :, 0:HD],
                                                    bank[6][:, t * D:(t + 1) * D].rearrange("p (h d) -> p h d", h=H),
                                                    rows[:, ROWS["bV"], :].rearrange("p (h d) -> p h d", h=H), ALU.add)
                        ins.then_inc(values_ready["att"], 1)
                    if n == 9 and routed:
                        after(dve, z_out, count(i, 2, 1, 1))
                        after(dve, h1b_ready, count(i, 2, 1, 1))
                        after(dve, out_stored, count(i, 2, DMA, DMA))
                        after(dve, scattered, count(i, 2, T * DMA, DMA))
                        dve.tensor_tensor(h2row[:, :, 0:D], bank[7].rearrange("p (t d) -> p t d", t=T), h1b[:],
                                          ALU.add).then_inc(h2_ready, 1)
                        after(dve, h2_ready, count(i, 2, 1, 1))
                    if n == 24 and routed:
                        moments("h2", h2row)
                    if n == 30 and routed:
                        after(dve, rstd_ready["h2"], count(i, 2, 1, 1))
                        dve.tensor_copy(h2row[:, :, D + 2], mv["h2"][:, :, 0])
                        dve.tensor_copy(h2row[:, :, D + 3], rstd["h2"][:])
                    if n == 32 and tok:
                        normalise_ctx("tok", i, 0, (5, 6))
                    if n == 34 and tok:
                        after(dve, gathered, count(i, 0, T * DMA, 2 * T * DMA))
                        if att:
                            after(dve, turned["att"], count(i, 1, 2 * G, 2 * G))
                        split(xq_parts, xg, x_split)
                    if n == 36 and tok:
                        after(dve, attn_out, count(i, 0, 1, 1))
                        for t in range(T):
                            ins = dve.tensor_tensor(resid[:, t, :].rearrange("p (h d) -> p h d", h=H),
                                                    bank[5][:, t * D:(t + 1) * D].rearrange("p (h d) -> p h d", h=H),
                                                    values["tok"][:, t, :, 0:HD], ALU.add)
                        ins.then_inc(x_added, 1)
                        after(dve, x_added, count(i, 0, 1, 1))
                        moments("x1", resid)
                    if n == 38 and routed:
                        after(dve, logits, count(i, 2, 1, 1))
                        dve.tensor_copy(lg[:], bank[5][:, 0:T * E].rearrange("p (t e) -> p t e", t=T)
                                        ).then_inc(logits_read, 1)
                        after(dve, logits_read, count(i, 2, 1, 1))
                        link(dve.tensor_reduce(lmax[:], lg[:], AX_X, ALU.max))
                        dve.tensor_tensor(lsh[:], lg[:], spread(lmax), ALU.subtract).then_inc(shifted, 1)
                        link(dve.tensor_tensor(eq[:], lg[:], spread(lmax), ALU.is_equal))
                        link(dve.tensor_tensor(eqr[:], eq[:], rev[:], ALU.mult))
                        link(dve.tensor_reduce(first[:], eqr[:], AX_X, ALU.max))
                        link(dve.tensor_tensor(onehot[:], eqr[:], spread(first), ALU.is_equal))
                        dve.tensor_copy(onehotb[:], onehot[:]).then_inc(onehot_ready, 1)
                    if n == 40 and routed:
                        after(dve, exped, count(i, 2, 1, 1))
                        link(dve.tensor_reduce(lsum[:], lexp[:], AX_X, ALU.add))
                        dve.reciprocal(h2row[:, :, D], lsum[:])
                    if n == 43 and routed:
                        after(dve, ranked, count(i, 2, 1, 1))
                        link(dve.tensor_tensor(posr[:], bank[7][:, 0:T * E].rearrange("p (t e) -> p t e", t=T),
                                               counts[:].rearrange("p (a e) -> p a e", a=1).to_broadcast([P, T, E]),
                                               ALU.add))
                        dve.tensor_tensor(counts[:], counts[:], bank[7][:, T * E:T * E + E],
                                          ALU.add).then_inc(ranks_read, 1)
                        link(dve.tensor_tensor(sel[:], onehot[:], posr[:], ALU.mult))
                        link(dve.tensor_reduce(locf[:], sel[:], AX_X, ALU.add))
                        dve.tensor_scalar(over[:], locf[:], float(CAP), float(NOWHERE), ALU.is_ge, ALU.mult)
                        link(dve.tensor_tensor(sel[:], onehot[:], ebase[:], ALU.mult))
                        link(dve.tensor_reduce(slotf[:], sel[:], AX_X, ALU.add))
                        link(dve.tensor_tensor(slotf[:], slotf[:], locf[:], ALU.add))
                        link(dve.tensor_tensor(slotf[:], slotf[:], over[:], ALU.add))
                        dve.tensor_copy(sloti[:], slotf[:]).then_inc(slot_ready, 1)
                    for pair_of in (1, 3):
                        if n == UP[pair_of][0] + 1 and tok:
                            relu(i, pair_of, UP[pair_of][1])
                    if n in ATT_TURN_SLOT and att:
                        m = ATT_TURN_SLOT.index(n)
                        if m % 2:
                            stack("att", i - 1, m, ATT_BANK[m])
                    if n in TOK_TURN_SLOT and tok:
                        m = TOK_TURN_SLOT.index(n)
                        if m % 2:
                            stack("tok", i + 1, m, TOK_BANK[m])
                return links[2] - at_start

            links[0] = 0
            dve.wait_ge(gathered, T * DMA)
            split(xq_parts, xg, x_split)
            for m in range(1, 2 * G, 2):
                stack("tok", 0, m, TOK_BANK[m])

            def vectored(i, on):
                if isinstance(i, int):
                    if i == B:
                        links[1], links[2] = 0, links[2] + (B - 2) * STEADY_VECTOR
                    iteration(i, on)
                else:
                    links[1], links[2] = STEADY_VECTOR, links[2] - 2 * STEADY_VECTOR
                    n = iteration(i, on)
                    assert n == STEADY_VECTOR, n
                    links[2] += STEADY_VECTOR

            iterations(dve, vectored)

            def prepare(e, k, loads):
                dve.wait_ge(e_loaded[k], loads * (5 * DMA))
                for t in range(CT):
                    ins = dve.tensor_scalar(xen[:, t, :], xe[:, k, t, 0:D], xe[:, k, t, D + 2:D + 3],
                                            xe[:, k, t, D + 3:D + 4], ALU.subtract, ALU.mult)
                ins.then_inc(e_normed, 1)
                dve.wait_ge(e_turned, e + 1)
                for c in range(C2):
                    ins = dve.tensor_copy(xeT[:, c, :], bank[c])
                ins.then_inc(eT_ready, 1)

            def expert(j, k, more):
                if more:
                    prepare(j * 2 + k + 1, 1 - k, j + k + 1)
                for t in range(CT):
                    n = j * (2 * CT) + k * CT + t + 1
                    dve.wait_ge(e_down, n)
                    dve.tensor_tensor(yb[:, t % 2, :], bank[6 + t % 2][:, 0:D], mb2_sb[:, k, :],
                                      ALU.add).then_inc(e_biased, 1)
                    dve.wait_ge(e_biased, n + 1)
                    dve.scalar_tensor_tensor(out=yo[:, k, t, :], in0=yb[:, t % 2, :], scalar=xe[:, k, t, D:D + 1],
                                             in1=xe[:, k, t, 0:D], op0=ALU.mult, op1=ALU.add).then_inc(e_out, 1)

            prepare(0, 0, 1)
            experts(dve, expert)

        @block.tensor
        def _(pe):
            def turn(k, tile, who):
                for c in range(C2):
                    for t in range(T):
                        ins = pe.transpose(bank[k][:, c * S + t * P:c * S + (t + 1) * P],
                                           tile[:, t, c * P:(c + 1) * P], ident[:])
                ins.then_inc(who, 1)

            def project(k, srcT, w, who):
                for t in range(T):
                    for c in range(C2):
                        ins = pe.matmul(bank[k][:, t * D:(t + 1) * D], srcT[:, c, t * P:(t + 1) * P], w[:, c, :],
                                        start=(c == 0), stop=(c == C2 - 1))
                ins.then_inc(who, 1)

            def turn_ctx(s, banks, who):
                for t in range(T):
                    for g in range(G):
                        ins = pe.transpose(bank[banks[t]][:, g * P:(g + 1) * P], CU[:, g, t * P:(t + 1) * P], ident[:])
                    ins.then_inc(who, 1)

            def turn_parts(s, i, m, k, left):
                if left:
                    turn_left(pe, s, i, 0, left - 1)
                parts = xq_parts if s == "tok" or m % 2 else k_parts
                for b in range(2):
                    block_of = 2 * (m // 2) + b
                    for t in range(T):
                        first_place = 1 if parts is xq_parts and m % 2 == 0 else 0
                        src = parts[:, t, block_of, first_place:first_place + 4, :].rearrange("p l w -> p (l w)")
                        ins = pe.transpose(bank[k][:, b * S + t * P:b * S + (t + 1) * P].bitcast(F32R), src, identr[:])
                ins.then_inc(turned[s], 1)

            def core(s, i, n):
                causal = s == "att"
                seq = i - 1 if causal else i
                if n in RING_SLOT:
                    place = RING_SLOT.index(n)
                    kind, index = RING[place]
                    tile = bank[place % 2]
                    before_kind, before_index = RING[place - 2]
                    if before_kind == "S":
                        after(pe, maxed, run_count(s, i, H, before_index + 1 - (H if place < 2 else 0)))
                    else:
                        after(pe, negT_ready, run_count(s, i, G, before_index + 1 - (G if place < 2 else 0)))
                    if kind == "S":
                        h = index
                        for turn_of in (2 * (h // 4), 2 * (h // 4) + 1):
                            turn_left(pe, s, seq, 0, turn_of)
                        for t in range(T):
                            col, keys = (t * P, (t + 1) * P) if causal else (t * S, S)
                            ins = pe.matmul(tile[:, col:col + keys], QS[s][:, h // 2, t * P:(t + 1) * P],
                                            KS[s][:, h // 2, h % 2, 0:keys], start=True, stop=not causal)
                            if causal:
                                d = col + t * P
                                ins = pe.matmul(tile[:, d:d + P], identb[:], maskq[:], start=False, stop=True)
                    else:
                        after(pe, neg_ready, run_count(s, i, G, index + 1))
                        for k, t in enumerate((1, 0, 1) if causal else (0, 1)):
                            ins = pe.transpose(tile[0:4, k * P:(k + 1) * P], negmax[:, t, 4 * index:4 * index + 4],
                                               ident[:])
                    ins.then_inc(ring_filled, 1)
                if n in TURNED_SLOT:
                    h = TURNED_SLOT.index(n)
                    g, r = h // 4, h % 4
                    tile = bank[2 + h % 2]
                    after(pe, negT_ready, run_count(s, i, G, g + 1))
                    after(pe, probs, run_count(s, i, H, h - 1))
                    if causal:
                        pe.matmul(tile[:, P:], identr[:, r:r + 1].to_broadcast([P, P]), negmaxT[:, g, :],
                                  start=True, stop=False, skip_group_check=True)
                    else:
                        pe.matmul(tile.rearrange("p (k q) -> p k q", k=T), identr[:, r:r + 1].to_broadcast([P, P]),
                                  negmaxT[:, g:g + 1, 0:S].to_broadcast([P, T, S]), start=True, stop=False,
                                  skip_group_check=True)
                    for kt in range(T):
                        q0 = kt * P if causal else 0
                        col = (T - 1 - kt) * S + q0 if causal else kt * S
                        ins = pe.matmul(tile[:, col:col + S - q0], KS[s][:, h // 2, h % 2, kt * P:(kt + 1) * P],
                                        QS[s][:, h // 2, q0:S], start=False, stop=not causal, skip_group_check=True)
                        if causal:
                            ins = pe.matmul(tile[:, col:col + P], identb[:], maskk[:], start=False, stop=True,
                                            skip_group_check=True)
                    ins.then_inc(scores, 1)
                if n in VALUE_SLOT:
                    g = VALUE_SLOT.index(n)
                    after(pe, values_ready[s], count(seq, 0, 1, 1))
                    after(pe, probs, run_count(s, i, H, 4 * g + 4))
                    after(pe, ctx_copied, run_count(s, i, G, g))
                    for kt in range(T):
                        q0 = kt * P if causal else 0
                        col = (T - 1 - kt) * S + q0 if causal else kt * S
                        for r in range(4):
                            ins = pe.matmul(bank[4][32 * r:32 * r + 32, q0:S], values[s][:, kt, 4 * g + r, :],
                                            prob[:, g % 2, r, col:col + S - q0],
                                            start=(kt == 0), stop=(kt == T - 1), skip_group_check=True)
                    ins.then_inc(ctx_done, 1)

            pe.wait_ge(ids_cleaned, 1)
            pe.transpose(bank[7][:, 0:NT], ids_f[:], ident[0:NT, 0:NT]).then_inc(ids_turned, 1)
            pe.wait_ge(ids_ready, 1)
            pe.wait_ge(x_parts, 1)
            for m in range(2 * G):
                turn_parts("tok", 0, m, TOK_BANK[m], TOK_LEFT[m])
            pe.wait_ge(loaded, N_LOADS * DMA)

            def iteration(i, on):
                tok, att, routed = on
                for n in range(SLOTS):
                    if tok:
                        core("tok", i, n)
                    if att:
                        core("att", i, n - ATT_SLOT)
                    if n == 0 and att:
                        turns_left(pe, "tok", i, 0)
                    if n in DOWN_SLOT and att:
                        t, half = divmod(DOWN_SLOT.index(n), 2)
                        if t and routed:
                            after(pe, ctx_normed["att"], count(i, 2, T, 1))
                        for f in range(half * NF // 2, (half + 1) * NF // 2):
                            if t == 0:
                                after(pe, relu_dve if f // 2 % 2 else relu_act, count(i, 1, 2, f // 4 + 1))
                            ins = pe.matmul(bank[(7, 5)[t]][:, 0:D], hid[:, f, t * P:(t + 1) * P], w2_sb[:, f, :],
                                            start=(f == 0), stop=(f == NF - 1))
                        if half:
                            ins.then_inc(down_done, 1)
                    if n == 1 and routed:
                        after(pe, ctx_copied, run_count("att", i - 1, G, G))
                        turn_ctx("att", (5, 6), ctx_turned["att"])
                    if n == 17 and att:
                        after(pe, h1_normed, count(i, 1, 1, 1))
                        turn(6, normed_h1, h1_turned)
                    if n == 18 and att:
                        after(pe, h1T_ready, count(i, 1, 1, 1))
                        if routed:
                            after(pe, h2_ready, count(i, 2, 1, 1))
                        project(7, h1T, wq_sb, q_proj)
                    if n == 19 and att:
                        project(5, h1T, wk_sb, k_proj)
                    if n == 20 and att:
                        project(6, h1T, wv_sb, v_proj)
                    if n in ATT_TURN_SLOT and att:
                        m = ATT_TURN_SLOT.index(n)
                        if m == 0:
                            after(pe, k_parted, count(i, 1, 1, 1))
                        if m == 1:
                            after(pe, q_parted, count(i, 1, 1, 1))
                        if m == 2:
                            after(pe, values_ready["att"], count(i, 1, 1, 1))
                        turn_parts("att", i - 1, m, ATT_BANK[m], ATT_LEFT[m])
                    if n == 6 and routed:
                        after(pe, z_ready, count(i, 2, 1, 1))
                        for t in range(T):
                            ins = pe.transpose(bank[6][0:HD, t * P:(t + 1) * P], zsum[:, t, :], ident[:])
                        ins.then_inc(z_turned, 1)
                    if n == 8 and routed:
                        if att:
                            after(pe, y_added, count(i, 1, T, 1))
                        else:
                            after(pe, ranks_read, count(i, 3, 1, 1))
                        after(pe, zT_ready, count(i, 2, 1, 1))
                        for t in range(T):
                            ins = pe.matmul(bank[7][:, t * D:(t + 1) * D], zT[:, t * P:(t + 1) * P], wo_sb[:],
                                            start=True, stop=True)
                        ins.then_inc(z_out, 1)
                    if n == 31 and tok:
                        after(pe, ctx_copied, run_count("tok", i, G, G))
                        if att:
                            turns_left(pe, "att", i, 1)
                        else:
                            turns_left(pe, "tok", i, 0)
                        turn_ctx("tok", (5, 6), ctx_turned["tok"])
                    if n == 34 and tok:
                        after(pe, ctx_normed["tok"], count(i, 0, T, T))
                        turn(7, ctxn[:].rearrange("p t h d -> p t (h d)"), ctxnT_turned)
                    if n == 35 and tok:
                        after(pe, ctxnT_ready, count(i, 0, 1, 1))
                        project(5, ctxnT, w_o_sb, attn_out)
                    if n == 33 and routed:
                        if att:
                            turns_left(pe, "att", i, 1)
                        if tok:
                            after(pe, ctx_normed["tok"], count(i, 0, T, T))
                        after(pe, h2_normed, count(i, 2, 1, 1))
                        turn(6, normed_h2, h2_turned)
                    if n == 37 and routed:
                        after(pe, h2T_ready, count(i, 2, 1, 1))
                        if tok:
                            after(pe, x_added, count(i, 0, 1, 1))
                        for t in range(T):
                            for c in range(C2):
                                ins = pe.matmul(bank[5][:, t * E:(t + 1) * E], h2T[:, c, t * P:(t + 1) * P],
                                                wg_sb[:, c, :], start=(c == 0), stop=(c == C2 - 1))
                        ins.then_inc(logits, 1)
                    if n in TOK_TURN_SLOT and tok:
                        m = TOK_TURN_SLOT.index(n)
                        if m == 0:
                            after(pe, x_parts, count(i, 0, 1, 2))
                        if m == 3 and routed:
                            after(pe, ranks_read, count(i, 2, 1, 1))
                        if m == 7:
                            after(pe, relu_act, count(i, 0, 2, 2))
                        turn_parts("tok", i + 1, m, TOK_BANK[m], TOK_LEFT[m])
                    if n == 42 and tok:
                        if routed:
                            after(pe, logits_read, count(i, 2, 1, 1))
                        after(pe, x1_normed, count(i, 0, 1, 1))
                        turn(5, normed, x1_turned)
                    for pair_of, (slot, k) in enumerate(UP):
                        if n == slot and tok:
                            if pair_of == 0:
                                after(pe, x1T_ready, count(i, 0, 1, 1))
                                turn_left(pe, "tok", i + 1, 0, 1)
                            if pair_of == 2:
                                after(pe, relu_act, count(i, 0, 2, 1))
                            if pair_of == 3:
                                after(pe, relu_dve, count(i, 0, 2, 1))
                            for f in (2 * pair_of, 2 * pair_of + 1):
                                for c in range(C2):
                                    ins = pe.matmul(bank[k][:, (f % 2) * S:(f % 2 + 1) * S],
                                                    w1_sb[:, c, f * P:(f + 1) * P], x1T[:, c, :],
                                                    start=(c == 0), stop=(c == C2 - 1))
                            ins.then_inc(up_done, 1)
                    if n == 41 and routed:
                        after(pe, onehot_ready, count(i, 2, 1, 1))
                        if tok:
                            turn_left(pe, "tok", i + 1, 0, 2)
                        pe.matmul(bank[7][:, 0:E], before[:], onehotb[:, 0, :], start=True, stop=True)
                        pe.matmul(bank[7][:, E:2 * E], before[:], onehotb[:, 1, :], start=True, stop=False)
                        pe.matmul(bank[7][:, E:2 * E], onesb[:], onehotb[:, 0, :], start=False, stop=True)
                        pe.matmul(bank[7][:, 2 * E:3 * E], onesb[:], onehotb[:, 0, :], start=True, stop=False)
                        pe.matmul(bank[7][:, 2 * E:3 * E], onesb[:], onehotb[:, 1, :], start=False, stop=True
                                  ).then_inc(ranked, 1)

            iterations(pe, iteration)

            def turn_tokens(e):
                pe.wait_ge(e_normed, e + 1)
                for c in range(C2):
                    for t in range(CT):
                        ins = pe.transpose(bank[c][:, t * P:(t + 1) * P], xen[:, t, c * P:(c + 1) * P], ident[:])
                ins.then_inc(e_turned, 1)

            def expert(j, k, more):
                e = j * 2 + k
                pe.wait_ge(eT_ready, e + 1)
                for f in range(NF):
                    if f >= 4:
                        pe.wait_ge(e_relu, j * (2 * NF) + k * NF + f - 3)
                    for c in range(C2):
                        ins = pe.matmul(bank[2 + f % 4], mw1[k][:, c, f * P:(f + 1) * P], xeT[:, c, :],
                                        start=(c == 0), stop=(c == C2 - 1))
                    ins.then_inc(e_up, 1)
                if more:
                    turn_tokens(e + 1)
                pe.wait_ge(e_relu, j * (2 * NF) + k * NF + NF)
                for t in range(CT):
                    if t >= 2:
                        pe.wait_ge(e_biased, j * (2 * CT) + k * CT + t)
                    else:
                        pe.wait_ge(e_biased, j * (2 * CT) + k * CT + 1)
                    for f in range(NF):
                        ins = pe.matmul(bank[6 + t % 2][:, 0:D], hid[:, f, t * P:(t + 1) * P], mw2[k][:, f, :],
                                        start=(f == 0), stop=(f == NF - 1))
                    ins.then_inc(e_down, 1)

            turn_tokens(0)
            experts(pe, expert)


_INS = ["x", "L0_tok_emb", "L0_tok_w_o", "L0_tok_w1", "L0_tok_b1", "L0_tok_w2", "L0_tok_b2", "L0_tok_gamma1",
        "L0_tok_beta1", "L0_tok_gamma2", "L0_tok_beta2", "L0_attn_WQ", "L0_attn_bQ", "L0_attn_WK", "L0_attn_bK",
        "L0_attn_WV", "L0_attn_bV", "L0_attn_WO", "L0_attn_bO", "L0_ffn_Wg", "L0_ffn_W1", "L0_ffn_b1",
        "L0_ffn_W2", "L0_ffn_b2"]
_OUTS = [((16, 256, 256), "float32")]


def kernel(**inputs):
    import numpy as _np
    import concourse.bacc as _bacc
    from concourse import mybir as _mybir
    from concourse.bass_utils import run_bass_kernel_spmd as _run

    nc = _bacc.Bacc("TRN2", target_bir_lowering=False, num_devices=1)
    arrays, args = {}, []
    for name in _INS:
        a = _np.ascontiguousarray(inputs[name])
        arrays[f"in_{name}_dram"] = a
        args.append(nc.dram_tensor(f"in_{name}_dram", a.shape, _mybir.dt.from_np(a.dtype), kind="ExternalInput").ap())
    for i, (shape, dtype) in enumerate(_OUTS):
        dt = _mybir.dt.from_np(_np.dtype(dtype))
        args.append(nc.dram_tensor(f"out_{i}_dram", shape, dt, kind="ExternalOutput").ap())
    lm_tower_kernel(nc, *args)
    r = _run(nc, [arrays], core_ids=[0])
    return r.results[0]["out_0_dram"]
```
